# Optimizing a Trainium2 kernel written in Bass

```python
import numpy as np
import jax
import jax.numpy as jnp

def _softmax(x, axis=-1):
    return jax.nn.softmax(x, axis=axis)

def _gelu(x):
    return jax.nn.gelu(x, approximate=True)

def _silu(x):
    return jax.nn.silu(x)

def _sigmoid(x):
    return jax.nn.sigmoid(x)

def _layernorm(x, axis=-1, eps=1e-05):
    m = jnp.mean(x, axis=axis, keepdims=True)
    v = jnp.var(x, axis=axis, keepdims=True)
    return (x - m) / jnp.sqrt(v + eps)

def _scatter_add(tgt, idx, src, axis=0):
    return tgt.at[idx].add(src)

def _segment_sum(src, seg, n):
    return jax.ops.segment_sum(src, seg, n)
kernel_name = 'mk_xattn_ffn_d1_seqx_r4_f5fc03'

def setup_inputs(seed: int=0):
    np.random.seed(seed)
    _w = jnp.asarray

    def _rec_inputs():
        import jax
        import jax.numpy as jnp
        _rk = jax.random.key(seed)
        x = -0.0002928 + 1 * jax.random.normal(jax.random.fold_in(_rk, 1), (8, 256, 512), jnp.float32)
        _lenS = 256 - jax.random.randint(jax.random.fold_in(_rk, 7), (8,), 0, max(1, 256 // 4) + 1, jnp.int32)
        _lenS2 = 256 - jax.random.randint(jax.random.fold_in(_rk, 8), (8,), 0, max(1, 256 // 4) + 1, jnp.int32)
        _ctx_2048P = jax.random.normal(jax.random.fold_in(_rk, 11), (8, 16, 512), jnp.float32)
        _ctx_2048c = jax.random.dirichlet(jax.random.fold_in(_rk, 511), 0.3 * jnp.ones((16,), jnp.float32), (8, 256))
        _ctx_2048t = jnp.einsum('bsk,bkd->bsd', _ctx_2048c, _ctx_2048P)
        _ctx_2048t = _ctx_2048t * jax.lax.rsqrt(jnp.mean(jnp.square(_ctx_2048t)) + 1e-12) * 0.953939
        ctx_2048 = -1.39393e-06 + 0.999914 * (_ctx_2048t + 0.3 * jax.random.normal(jax.random.fold_in(_rk, 611), (8, 256, 512), jnp.float32))
        return (x, ctx_2048)
    x, ctx_2048 = _rec_inputs()

    def _L0_xattn_setup():
        import jax, jax.numpy as jnp
        import numpy as np
        B, S, E, NH = (2, 256, 512, 16)
        DH = E // NH
        EPS = 1e-06

        def _mlstm_forward(q, k, v, Wi, bi, Wf, bf, ln_scale):
            b, s, e = q.shape
            nh = Wi.shape[1]
            dh = e // nh
            x = jnp.concatenate([q, k, v], axis=-1)
            ig = (x @ Wi + bi).transpose(0, 2, 1)[..., None]
            fg = (x @ Wf + bf).transpose(0, 2, 1)[..., None]
            split = lambda t: t.reshape(b, s, nh, dh).transpose(0, 2, 1, 3)
            qh, kh, vh = (split(q), split(k), split(v))
            log_f = jax.nn.log_sigmoid(fg)
            log_f_cum = jnp.concatenate([jnp.zeros((b, nh, 1, 1), q.dtype), jnp.cumsum(log_f, axis=2)], axis=2)
            fg_mat = log_f_cum - jnp.transpose(log_f_cum, (0, 1, 3, 2))
            ltr = jnp.tril(jnp.ones((s, s), dtype=bool))
            log_fg = jnp.where(ltr, fg_mat[:, :, 1:, 1:], -jnp.inf)
            log_D = log_fg + jnp.transpose(ig, (0, 1, 3, 2))
            max_log_D = jnp.max(log_D, axis=-1, keepdims=True)
            D = jnp.exp(log_D - max_log_D)
            qk = jnp.einsum('bhsd,bhtd->bhst', qh, kh) / jnp.sqrt(jnp.asarray(dh, q.dtype))
            C = qk * D
            normalizer = jnp.maximum(jnp.abs(C.sum(-1, keepdims=True)), jnp.exp(-max_log_D))
            Cn = C / (normalizer + EPS)
            h = jnp.einsum('bhst,bhtd->bhsd', Cn, vh)
            mu = h.mean(-1, keepdims=True)
            var = ((h - mu) ** 2).mean(-1, keepdims=True)
            hn = (h - mu) * jax.lax.rsqrt(var + EPS)
            hn = hn * ln_scale.reshape(1, nh, 1, dh)
            return hn.transpose(0, 2, 1, 3).reshape(b, s, e)
        key = jax.random.key(seed)
        ks = jax.random.split(key, 6)
        q = jax.random.normal(ks[0], (B, S, E), dtype=jnp.float32)
        k = jax.random.normal(ks[1], (B, S, E), dtype=jnp.float32)
        v = jax.random.normal(ks[2], (B, S, E), dtype=jnp.float32)
        Wi = jax.random.normal(ks[3], (3 * E, NH), dtype=jnp.float32) * 0.02
        bi = jax.random.normal(ks[4], (NH,), dtype=jnp.float32) * 0.1
        Wf = jax.random.normal(ks[5], (3 * E, NH), dtype=jnp.float32) * 0.02
        bf = jnp.linspace(3.0, 6.0, NH, dtype=jnp.float32)
        ln_scale = jnp.ones((E,), dtype=jnp.float32)
        return {'q': q, 'k': k, 'v': v, 'Wi': Wi, 'bi': bi, 'Wf': Wf, 'bf': bf, 'ln_scale': ln_scale}
    _L0_xattn_all = _L0_xattn_setup()
    _L0_xattn_in = {k: v for k, v in _L0_xattn_all.items() if k in ('Wi', 'bi', 'Wf', 'bf', 'ln_scale')}
    del _L0_xattn_all

    def _L0_ffn_setup():
        import jax, jax.numpy as jnp
        import numpy as np
        _FP4_LUT = jnp.array([0.0, 0.5, 1.0, 1.5, 2.0, 3.0, 4.0, 6.0, -0.0, -0.5, -1.0, -1.5, -2.0, -3.0, -4.0, -6.0], dtype=jnp.float32)
        GROUP_SIZE = 128
        EPS = 1e-06

        def _dequant_fp4(packed_i32, scales_f16, group_size):
            out_f, in_p = packed_i32.shape
            w = packed_i32.astype(jnp.uint32)
            shifts = jnp.arange(8, dtype=jnp.uint32) * 4
            nib = w[:, :, None] >> shifts & jnp.uint32(15)
            vals = _FP4_LUT[nib.astype(jnp.int32)].reshape(out_f, in_p * 8)
            s = scales_f16.astype(jnp.float32).T
            s_full = jnp.repeat(s, group_size, axis=1)
            return vals * s_full
        key = jax.random.key(seed)
        k1, k2, k3, k4, k5 = jax.random.split(key, 5)
        B, S, H, I = (4, 512, 512, 1408)
        x = jax.random.normal(k1, (B, S, H), dtype=jnp.float32)
        gate_up_packed = jax.random.randint(k2, (2 * I, H // 8), 0, 2147483647, dtype=jnp.int32)
        gate_up_scales = jax.random.uniform(k3, (H // GROUP_SIZE, 2 * I), dtype=jnp.float32).astype(jnp.float16)
        down_packed = jax.random.randint(k4, (H, I // 8), 0, 2147483647, dtype=jnp.int32)
        down_scales = jax.random.uniform(k5, (I // GROUP_SIZE, H), dtype=jnp.float32).astype(jnp.float16)
        return {'x': x, 'gate_up_packed': gate_up_packed, 'gate_up_scales': gate_up_scales, 'down_packed': down_packed, 'down_scales': down_scales}
    _L0_ffn_all = _L0_ffn_setup()
    _L0_ffn_in = {k: v for k, v in _L0_ffn_all.items() if k in ('gate_up_packed', 'gate_up_scales', 'down_packed', 'down_scales')}
    del _L0_ffn_all
    return {'x': x, 'ctx_2048': ctx_2048, 'L0_xattn_Wi': _L0_xattn_in['Wi'], 'L0_xattn_bi': _L0_xattn_in['bi'], 'L0_xattn_Wf': _L0_xattn_in['Wf'], 'L0_xattn_bf': _L0_xattn_in['bf'], 'L0_xattn_ln_scale': _L0_xattn_in['ln_scale'], 'L0_ffn_gate_up_packed': _L0_ffn_in['gate_up_packed'], 'L0_ffn_gate_up_scales': _L0_ffn_in['gate_up_scales'], 'L0_ffn_down_packed': _L0_ffn_in['down_packed'], 'L0_ffn_down_scales': _L0_ffn_in['down_scales']}

def reference(x, ctx_2048, L0_xattn_Wi, L0_xattn_bi, L0_xattn_Wf, L0_xattn_bf, L0_xattn_ln_scale, L0_ffn_gate_up_packed, L0_ffn_gate_up_scales, L0_ffn_down_packed, L0_ffn_down_scales):
    import jax
    import jax.numpy as jnp

    def _L0_xattn_ref(q, k, v, Wi, bi, Wf, bf, ln_scale):
        import jax, jax.numpy as jnp
        import numpy as np
        B, S, E, NH = (2, 256, 512, 16)
        DH = E // NH
        EPS = 1e-06

        def _mlstm_forward(q, k, v, Wi, bi, Wf, bf, ln_scale):
            b, s, e = q.shape
            nh = Wi.shape[1]
            dh = e // nh
            x = jnp.concatenate([q, k, v], axis=-1)
            ig = (x @ Wi + bi).transpose(0, 2, 1)[..., None]
            fg = (x @ Wf + bf).transpose(0, 2, 1)[..., None]
            split = lambda t: t.reshape(b, s, nh, dh).transpose(0, 2, 1, 3)
            qh, kh, vh = (split(q), split(k), split(v))
            log_f = jax.nn.log_sigmoid(fg)
            log_f_cum = jnp.concatenate([jnp.zeros((b, nh, 1, 1), q.dtype), jnp.cumsum(log_f, axis=2)], axis=2)
            fg_mat = log_f_cum - jnp.transpose(log_f_cum, (0, 1, 3, 2))
            ltr = jnp.tril(jnp.ones((s, s), dtype=bool))
            log_fg = jnp.where(ltr, fg_mat[:, :, 1:, 1:], -jnp.inf)
            log_D = log_fg + jnp.transpose(ig, (0, 1, 3, 2))
            max_log_D = jnp.max(log_D, axis=-1, keepdims=True)
            D = jnp.exp(log_D - max_log_D)
            qk = jnp.einsum('bhsd,bhtd->bhst', qh, kh) / jnp.sqrt(jnp.asarray(dh, q.dtype))
            C = qk * D
            normalizer = jnp.maximum(jnp.abs(C.sum(-1, keepdims=True)), jnp.exp(-max_log_D))
            Cn = C / (normalizer + EPS)
            h = jnp.einsum('bhst,bhtd->bhsd', Cn, vh)
            mu = h.mean(-1, keepdims=True)
            var = ((h - mu) ** 2).mean(-1, keepdims=True)
            hn = (h - mu) * jax.lax.rsqrt(var + EPS)
            hn = hn * ln_scale.reshape(1, nh, 1, dh)
            return hn.transpose(0, 2, 1, 3).reshape(b, s, e)
        return _mlstm_forward(q, k, v, Wi, bi, Wf, bf, ln_scale)

    def _L0_ffn_ref(x, gate_up_packed, gate_up_scales, down_packed, down_scales):
        import jax, jax.numpy as jnp
        import numpy as np
        _FP4_LUT = jnp.array([0.0, 0.5, 1.0, 1.5, 2.0, 3.0, 4.0, 6.0, -0.0, -0.5, -1.0, -1.5, -2.0, -3.0, -4.0, -6.0], dtype=jnp.float32)
        GROUP_SIZE = 128
        EPS = 1e-06

        def _dequant_fp4(packed_i32, scales_f16, group_size):
            out_f, in_p = packed_i32.shape
            w = packed_i32.astype(jnp.uint32)
            shifts = jnp.arange(8, dtype=jnp.uint32) * 4
            nib = w[:, :, None] >> shifts & jnp.uint32(15)
            vals = _FP4_LUT[nib.astype(jnp.int32)].reshape(out_f, in_p * 8)
            s = scales_f16.astype(jnp.float32).T
            s_full = jnp.repeat(s, group_size, axis=1)
            return vals * s_full
        I = gate_up_packed.shape[0] // 2
        w_gu = _dequant_fp4(gate_up_packed, gate_up_scales, GROUP_SIZE)
        w_down = _dequant_fp4(down_packed, down_scales, GROUP_SIZE)
        gate_up = jnp.einsum('bsh,oh->bso', x, w_gu)
        gate, up = (gate_up[..., :I], gate_up[..., I:])
        h = jax.nn.silu(gate) * up
        y = jnp.einsum('bsi,hi->bsh', h, w_down)
        rms = jnp.sqrt(jnp.mean(y * y, axis=-1, keepdims=True) + EPS)
        return y / rms
    x = x + _L0_xattn_ref(_layernorm(x, axis=-1), ctx_2048, ctx_2048, L0_xattn_Wi, L0_xattn_bi, L0_xattn_Wf, L0_xattn_bf, L0_xattn_ln_scale)
    x = x + _L0_ffn_ref(_layernorm(x, axis=-1), L0_ffn_gate_up_packed, L0_ffn_gate_up_scales, L0_ffn_down_packed, L0_ffn_down_scales)
    return x

_drawn_inputs = setup_inputs


def setup_inputs(seed=0):
    import zlib

    import numpy as np

    out = dict(_drawn_inputs(seed))
    spreads = {'L0_xattn_ln_scale': (1.0, 0.2)}
    factors = {'L0_xattn_bi': 64.0}
    for name, (base, spread) in spreads.items():
        noise = np.random.default_rng([zlib.crc32(name.encode()), seed]).standard_normal(out[name].shape)
        drawn = base * np.exp(spread * noise) if base else spread * noise
        out[name] = jnp.asarray(drawn.astype(out[name].dtype))
    for name, factor in factors.items():
        out[name] = (out[name] * factor).astype(out[name].dtype)
    return out
```

```python
from contextlib import ExitStack

import concourse.bass as bass
from concourse import mybir

F32 = mybir.dt.float32
F16 = mybir.dt.float16
I32 = mybir.dt.int32
ALU = mybir.AluOpType
ACT = mybir.ActivationFunctionType
AX = mybir.AxisListType

P = 128
B, S, E, NH = 8, 256, 512, 16
DH = E // NH
PAIRS = B // 2
TT = 2 * S // P
KT = E // P
HG = P // DH
I = 1408
FT = I // P
GU = 2 * FT
NW = E // 8
DW = I // 8
UNITS = 2 * KT
PX = 1024.0
EPS_LN = 1e-5
EPS = 1e-6
FP4_SCALE = 16384.0
SIGN_MASK = 0x80008000 - (1 << 32)
MAGN_MASK = 0x0E000E00


class Chain:

    def __init__(self, eng, sem):
        self.eng, self.sem, self.per, self.n, self.base = eng, sem, None, 0, 0

    def start(self, p):
        if self.per is None and self.n:
            self.per = self.n
        self.base = 0 if self.per is None else p * self.per
        self.n = 0

    def inc(self, ins):
        ins.then_inc(self.sem, 1)
        self.n += 1

    def wait(self):
        self.eng.wait_ge(self.sem, self.base + self.n)

    def link(self, ins):
        self.inc(ins)
        self.wait()


def xattn_ffn(nc, x, ctx, Wi, bi, Wf, bf, ln_scale, gu_packed, gu_scales, dn_packed, dn_scales, out):
    x_pairs = x.rearrange("(p b) (c q) d -> p q (b c) d", b=2, q=P)
    ctx_pairs = ctx.rearrange("(p b) (c q) d -> p q (b c) d", b=2, q=P)
    out_pairs = out.rearrange("(p b) (c q) d -> p q (b c) d", b=2, q=P)
    negm_dram = nc.dram_tensor("negm_dram", (2 * NH, S), F32, kind="Internal").ap()

    es = ExitStack()
    with es:
        def sb(name, shape, dt=F32):
            return es.enter_context(nc.sbuf_tensor(name, shape, dt))

        def sem(name):
            return es.enter_context(nc.semaphore(name))

        ident = sb("ident", [P, P])
        ident16 = sb("ident16", [P, P], F16)
        head_rows = sb("head_rows", [P, HG])
        neghalf = sb("neghalf", [P, TT * NH])
        bias_row = sb("bias_row", [P, 2 * NH])
        ln_row = sb("ln_row", [P, E])
        w_gate = sb("w_gate", [P, 12, 2 * NH])
        gu_val = sb("gu_val", [P, GU, KT, P], F16)
        w_down = sb("w_down", [P, FT, E])
        gu_scale = sb("gu_scale", [P, KT * GU])
        dn_scale = sb("dn_scale", [P, FT * KT])
        sc_raw = sb("sc_raw", [KT * GU, P], F16)
        dsc_raw = sb("dsc_raw", [FT * KT, P], F16)
        x_sb = sb("x_sb", [P, TT, E])
        x_res = sb("x_res", [P, TT, E])
        ctx_sb = sb("ctx_sb", [P, TT, E])
        tok = sb("tok", [P, TT, NH, DH + 1])
        xT = sb("xT", [P, 2 * KT, TT * P])
        v_sb = sb("v_sb", [P, TT, NH, DH + 1])
        q_diag = sb("q_diag", [P, 2, HG, TT * P])
        negm = sb("negm", [P, 4, HG, S])
        dmat = sb("dmat", [P, 2, 3, HG, P])
        yT = sb("yT", [P, 2, KT, TT * P], F16)
        ffn = sb("ffn", [P, 8, TT * P])
        th = sb("th", [P, 2, TT * P])
        hT = sb("hT", [P, FT, TT * P])
        g_sb = sb("g_sb", [P, 2, 2, 2, NH])
        gates = negm[0:2 * NH, 2, 0:2]
        lf = negm[0:2 * NH, 3]
        am = sb("am", [2 * NH, 2, S])
        nm = sb("nm", [2 * NH, S])
        aT = sb("aT", [P, 2, 2 * NH])
        floor = sb("floor", [P, 2, 2, NH])
        bst = sb("bst", [P, 2, TT, 6])
        mv = sb("mv", [P, 2, TT, 2])
        vv = sb("vv", [P, 2, TT])
        rs = sb("rs", [P, 2, TT])
        rk = sb("rk", [P, TT])
        vmean = sb("vmean", [P, 2, TT * NH])
        hn = sb("hn", [P, 4, TT * NH])
        hr = sb("hr", [P, TT * NH])
        ssq = sb("ssq", [P, TT])
        ms = sb("ms", [P, TT])
        yr = sb("yr", [P, TT])
        gu_words = x_res[:].rearrange("p a b -> p (a b)").bitcast(I32)[:, 0:GU * NW].rearrange(
            "p (o w) -> p o w", o=GU)
        dn_words = th[:].rearrange("p a b -> p (a b)").bitcast(I32)[:, 0:KT * DW].rearrange(
            "p (o w) -> p o w", o=KT)
        bits = yT[:].rearrange("p a b c -> p (a b c)").bitcast(I32)
        gu_bits = hT[:].rearrange("p a b -> p (a b)").bitcast(I32).rearrange(
            "p (o w i) -> p o w i", o=GU, i=4)
        gu_fp4 = hT[:].rearrange("p a b -> p (a b)").bitcast(F16).rearrange(
            "p (o k) -> p o k", o=GU)
        dn_bits = ffn[:].rearrange("p a b -> p (a b)").bitcast(I32)[:, 0:KT * 4 * DW].rearrange(
            "p (o w i) -> p o w i", o=KT, i=4)
        dn_fp4 = ffn[:].rearrange("p a b -> p (a b)").bitcast(F16)[:, 0:KT * I].rearrange(
            "p (o g w i h) -> p o i g w h", o=KT, g=FT, i=4, h=2)
        dn_f32 = hT[:].rearrange("p a b -> p (a b)").rearrange("p (o k) -> p o k", o=KT)
        xn = tok[:].rearrange("p a b c -> p a (b c)")[:, :, 0:E]
        osq = dmat[:].rearrange("p a b c d -> p (a b c d)")[:, 0:TT * E].rearrange(
            "p (g d) -> p g d", d=DH)

        pf = es.enter_context(nc.psum_tensor("pf", [P, 4, 512], F32))
        pq = es.enter_context(nc.psum_tensor("pq", [P, 2, 512], F32))
        po = es.enter_context(nc.psum_tensor("po", [P, 512], F32))
        pm = es.enter_context(nc.psum_tensor("pm", [P, 512], F32))

        s_const = sem("s_const")
        s_words = sem("s_words")
        s_x = sem("s_x")
        s_ctx = sem("s_ctx")
        s_res = sem("s_res")
        s_nm = sem("s_nm")
        s_negm = [sem(f"s_negm{i}") for i in range(4)]
        s_out = sem("s_out")
        const_ready = sem("const_ready")
        wg_ready = sem("wg_ready")
        sc_done = sem("sc_done")
        sc_ready = sem("sc_ready")
        fp4_ready = sem("fp4_ready")
        gut_done = sem("gut_done")
        gut_read = sem("gut_read")
        dn32_ready = sem("dn32_ready")
        dnt_done = sem("dnt_done")
        dnt_read = sem("dnt_read")
        waits_taken = sem("waits_taken")
        dve_w = sem("dve_w")
        dve_a = sem("dve_a")
        act_a = sem("act_a")
        pool_a = sem("pool_a")
        var1_ready = sem("var1_ready")
        rstd1_ready = sem("rstd1_ready")
        xn_ready = sem("xn_ready")
        vmean_ready = sem("vmean_ready")
        v_ready = sem("v_ready")
        xT_done = sem("xT_done")
        xT_read = sem("xT_read")
        g_done = sem("g_done")
        g_ready = sem("g_ready")
        gT_done = sem("gT_done")
        absf_ready = sem("absf_ready")
        softp_ready = sem("softp_ready")
        nm_ready = sem("nm_ready")
        am_ready = sem("am_ready")
        back_done = sem("back_done")
        aT_ready = sem("aT_ready")
        floor_ready = sem("floor_ready")
        qdiag_ready = sem("qdiag_ready")
        qk_done = sem("qk_done")
        exp_done = sem("exp_done")
        mask_done = sem("mask_done")
        prod_done = sem("prod_done")
        pv_done = sem("pv_done")
        o_read = sem("o_read")
        osq_ready = sem("osq_ready")
        hvar_ready = sem("hvar_ready")
        hrstd_ready = sem("hrstd_ready")
        ols_ready = sem("ols_ready")
        x1_ready = sem("x1_ready")
        var2_ready = sem("var2_ready")
        rstd2_ready = sem("rstd2_ready")
        yn_ready = sem("yn_ready")
        yT_done = sem("yT_done")
        yh_ready = sem("yh_ready")
        yl_ready = sem("yl_ready")
        pu_done = sem("pu_done")
        t_ready = sem("t_ready")
        tsum_ready = sem("tsum_ready")
        acc_ready = sem("acc_ready")
        th_ready = sem("th_ready")
        gg_ready = sem("gg_ready")
        h_ready = sem("h_ready")
        dn_done = sem("dn_done")
        ss_ready = sem("ss_ready")
        ms_ready = sem("ms_ready")
        yr_ready = sem("yr_ready")
        o_ready = sem("o_ready")

        def take_wait(eng):
            eng.sem_inc(waits_taken, 1)

        block = es.enter_context(nc.Block())

        @block.sync
        def _(sp):
            def load_tokens(p):
                sp.dma_start(x_sb[:], x_pairs[p]).then_inc(s_x, 16)
                sp.dma_start(ctx_sb[:], ctx_pairs[p]).then_inc(s_ctx, 16)

            def keep_residual(q):
                sp.wait_ge(yn_ready, q + 1)
                take_wait(sp)
                sp.wait_ge(x1_ready, 4 * q + 4)
                take_wait(sp)
                sp.dma_start(x_res[:], x_sb[:]).then_inc(s_res, 16)
                sp.wait_ge(s_res, 16 * q + 16)
                take_wait(sp)

            def spread_negm(p):
                sp.wait_ge(nm_ready, p + 1)
                take_wait(sp)
                sp.wait_ge(am_ready, 2 * p + 2)
                take_wait(sp)
                if not (isinstance(p, int) and p == 0):
                    sp.wait_ge(exp_done, UNITS * p)
                sp.dma_start(negm_dram, nm[:]).then_inc(s_nm, 16)
                sp.wait_ge(s_nm, 16 * p + 16)
                take_wait(sp)
                for u in range(UNITS):
                    hg, b = u // 2, u % 2
                    if u >= 4:
                        sp.wait_ge(exp_done, UNITS * p + u - 3)
                    r = b * NH + hg * HG
                    sp.dma_start(negm[:, u % 4].rearrange("q h s -> q (h s)"),
                                 negm_dram[r:r + HG, :].rearrange("h s -> (h s)").partition_broadcast(P)
                                 ).then_inc(s_negm[u % 4], 16)

            def store(q):
                for tt in range(TT):
                    sp.wait_ge(o_ready, TT * q + tt + 1)
                    sp.dma_start(out_pairs[q][:, tt], x_res[:, tt]).then_inc(s_out, 16)
                sp.wait_ge(s_out, 16 * TT * q + 16 * TT)
                take_wait(sp)

            load_tokens(0)
            for i, w in enumerate((Wi, Wf)):
                sp.dma_start(w_gate[:, :, i * NH:(i + 1) * NH], w.rearrange("(k q) h -> q k h", q=P)
                             ).then_inc(s_const, 16)
            for i, v in enumerate((bi, bf)):
                sp.dma_start(bias_row[:, i * NH:(i + 1) * NH], v.partition_broadcast(P)
                             ).then_inc(s_const, 16)
            sp.dma_start(ln_row[:], ln_scale.partition_broadcast(P)).then_inc(s_const, 16)
            sp.dma_start(sc_raw[:], gu_scales.rearrange("g (o q) -> (g o) q", q=P)).then_inc(s_const, 16)
            sp.dma_start(dsc_raw[:], dn_scales.rearrange("g (o q) -> (g o) q", q=P)).then_inc(s_const, 16)
            sp.dma_start(gu_words, gu_packed.rearrange("(o q) w -> q o w", q=P)).then_inc(s_words, 16)
            sp.dma_start(dn_words, dn_packed.rearrange("(o q) w -> q o w", q=P)).then_inc(s_words, 16)
            spread_negm(0)
            sp.wait_ge(fp4_ready, 3)
            with sp.Fori(1, PAIRS) as p:
                keep_residual(p - 1)
                load_tokens(p)
                spread_negm(p)
                store(p - 1)
            keep_residual(PAIRS - 1)
            store(PAIRS - 1)

        @block.gpsimd
        def _(pool):
            chain = Chain(pool, pool_a)

            def setup():
                pool.memset(ident[:], 0.0).then_inc(const_ready, 1)
                pool.wait_ge(const_ready, 1)
                pool.affine_select(out=ident[:], in_=ident[:], compare_op=ALU.not_equal, fill=1.0, base=0,
                                   pattern=[[-1, P]], channel_multiplier=1).then_inc(const_ready, 1)
                pool.wait_ge(const_ready, 2)
                pool.tensor_copy(ident16[:], ident[:]).then_inc(const_ready, 1)
                pool.memset(neghalf[:], -0.5).then_inc(const_ready, 1)
                pool.memset(v_sb[:, :, :, DH:DH + 1], 1.0).then_inc(const_ready, 1)
                pool.memset(head_rows[:], 1.0).then_inc(const_ready, 1)
                pool.wait_ge(const_ready, 6)
                pool.affine_select(out=head_rows[:], in_=head_rows[:], compare_op=ALU.is_ge, fill=0.0,
                                   base=0, pattern=[[-DH, HG]], channel_multiplier=1
                                   ).then_inc(const_ready, 1)
                pool.wait_ge(const_ready, 7)
                pool.affine_select(out=head_rows[:], in_=head_rows[:], compare_op=ALU.is_ge, fill=0.0,
                                   base=DH - 1, pattern=[[DH, HG]], channel_multiplier=-1
                                   ).then_inc(const_ready, 1)
                pool.wait_ge(const_ready, 8)

            def norm1(p):
                pool.wait_ge(var1_ready, p + 1)
                pool.tensor_tensor(rs[:, 0], vv[:, 0], neghalf[:, 0:TT], ALU.pow).then_inc(rstd1_ready, 1)
                pool.wait_ge(vmean_ready, p + 1)
                pool.wait_ge(s_ctx, 16 * p + 16)
                if not (isinstance(p, int) and p == 0):
                    pool.wait_ge(pv_done, UNITS * p)
                for tt in range(TT):
                    m = vmean[:, 1, tt * NH:(tt + 1) * NH].unsqueeze(2).to_broadcast([P, NH, DH])
                    pool.tensor_tensor(v_sb[:, tt, :, 0:DH],
                                       ctx_sb[:, tt].rearrange("q (h d) -> q h d", d=DH), m, ALU.add
                                       ).then_inc(v_ready, 1)

            def spread_q(p, hg):
                pool.wait_ge(xT_read, 2 * KT * p + hg + 1)
                if hg >= 2:
                    pool.wait_ge(qk_done, 3 * UNITS * p + 6 * (hg - 1))
                elif not (isinstance(p, int) and p == 0):
                    pool.wait_ge(qk_done, 3 * UNITS * p)
                take_wait(pool)
                for h in range(HG):
                    pool.tensor_scalar(q_diag[:, hg % 2, h], xT[:, hg], head_rows[:, h:h + 1], None,
                                       ALU.mult).then_inc(qdiag_ready, 1)

            def mask(p, u):
                pool.wait_ge(exp_done, UNITS * p + u + 1)
                take_wait(pool)
                for blk in (0, 2):
                    d = dmat[:, u % 2, blk]
                    pool.affine_select(out=d, in_=d, compare_op=ALU.is_ge, fill=0.0, base=0,
                                       pattern=[[0, HG], [1, P]], channel_multiplier=-1
                                       ).then_inc(mask_done, 1)

            def post(p):
                pool.wait_ge(o_read, UNITS * p + UNITS)
                pool.wait_ge(osq_ready, p + 1)
                if isinstance(p, int) and p == 0:
                    pool.wait_ge(s_const, 16 * 7)
                for tt in range(TT):
                    o = tok[:, tt, :, 0:DH]
                    pool.tensor_tensor(o, o, ln_row[:].rearrange("q (h d) -> q h d", d=DH), ALU.mult
                                       ).then_inc(ols_ready, 1)
                pool.wait_ge(hvar_ready, p + 1)
                pool.tensor_tensor(hr[:], hn[:, 3], neghalf[:], ALU.pow).then_inc(hrstd_ready, 1)

            def norm2(p):
                pool.wait_ge(var2_ready, p + 1)
                pool.tensor_tensor(rs[:, 1], vv[:, 1], neghalf[:, 0:TT], ALU.pow).then_inc(rstd2_ready, 1)

            def ffn_up(q, j):
                for w in range(2):
                    n = 2 * j + w
                    pool.wait_ge(t_ready, 4 * FT * q + 2 * n + 2)
                    t = ffn[:, 2 * (n % 2)]
                    pool.tensor_tensor(t, t, ffn[:, 2 * (n % 2) + 1], ALU.add).then_inc(tsum_ready, 1)
                pool.wait_ge(acc_ready, 4 * FT * q + 4 * j + 4)
                pool.wait_ge(gg_ready, FT * q + j + 1)
                pool.tensor_tensor(hT[:, j], ffn[:, 6 + j % 2], th[:, j % 2], ALU.mult
                                   ).then_inc(h_ready, 1)

            def down(q, half):
                pool.wait_ge(ms_ready, 2 * q + half + 1)
                c = slice(2 * half, 2 * half + 2)
                pool.tensor_tensor(yr[:, c], ms[:, c], neghalf[:, c], ALU.pow).then_inc(yr_ready, 1)

            def iteration(p, q):
                for j in range(FT):
                    if q is not None:
                        ffn_up(q, j)
                    if p is not None:
                        if j == 1:
                            norm1(p)
                            spread_q(p, 0)
                            spread_q(p, 1)
                        if 4 < j and j - 5 < UNITS:
                            mask(p, j - 5)
                            if j - 5 in (1, 3):
                                spread_q(p, 2 + (j - 6) // 2)
                if p is not None:
                    mask(p, 6)
                if q is not None:
                    down(q, 0)
                if p is not None:
                    mask(p, 7)
                    post(p)
                    norm2(p)
                if q is not None:
                    down(q, 1)

            setup()
            iteration(0, None)
            with pool.Fori(1, PAIRS) as p:
                iteration(p, p - 1)
            iteration(None, PAIRS - 1)

        @block.scalar
        def _(act):
            chain = Chain(act, act_a)

            def read_xT(p):
                for n in range(2 * KT):
                    act.wait_ge(xT_done, 2 * KT * p + n + 1)
                    if n == 0 and not (isinstance(p, int) and p == 0):
                        act.wait_ge(qdiag_ready, NH * p)
                        act.wait_ge(qk_done, 3 * UNITS * p)
                    act.activation(xT[:, n], pq[:, n % 2], ACT.Copy).then_inc(xT_read, 1)

            def softplus(p):
                act.wait_ge(absf_ready, p + 1)
                chain.link(act.activation(lf[:, 1], lf[:, 0], ACT.Exp, scale=-1.0))
                act.activation(lf[:, 2], lf[:, 1], ACT.Ln, bias=1.0).then_inc(softp_ready, 1)

            def floors(p):
                act.wait_ge(aT_ready, p + 1)
                if not (isinstance(p, int) and p == 0):
                    act.wait_ge(hvar_ready, p)
                act.activation(floor[:].rearrange("q b c h -> q c b h"),
                               pm[:, 4 * NH:8 * NH].rearrange("q (c b h) -> q c b h", c=2, b=2),
                               ACT.Exp).then_inc(floor_ready, 1)

            def exps(p, u):
                hg, b = u // 2, u % 2
                act.wait_ge(s_negm[u % 4], 32 * p + 16 * (u // 4) + 16)
                act.wait_ge(aT_ready, p + 1)
                if u >= 2:
                    act.wait_ge(pv_done, UNITS * p + u - 1)
                elif not (isinstance(p, int) and p == 0):
                    act.wait_ge(hvar_ready, p)
                for h in range(HG):
                    bh = b * NH + hg * HG + h
                    act.activation(dmat[:, u % 2, 0:2, h],
                                   negm[:, u % 4, h].rearrange("q (c s) -> q c s", c=2), ACT.Exp,
                                   bias=aT[:, 0, bh:bh + 1])
                    last = act.activation(dmat[:, u % 2, 2, h], negm[:, u % 4, h, P:S], ACT.Exp,
                                          bias=aT[:, 1, bh:bh + 1])
                last.then_inc(exp_done, 1)

            def read_o(p, u):
                hg, b = u // 2, u % 2
                act.wait_ge(pv_done, UNITS * p + u + 1)
                act.activation(tok[:, 2 * b:2 * b + 2, hg * HG:(hg + 1) * HG, :].rearrange(
                                   "q c h d -> q c (h d)"),
                               po[:, 0:2 * HG * (DH + 1)].rearrange("q (c n) -> q c n", c=2),
                               ACT.Copy).then_inc(o_read, 1)

            def squares(p):
                act.wait_ge(o_read, UNITS * p + UNITS)
                act.wait_ge(pv_done, UNITS * p + UNITS)
                act.activation(osq, tok[:].rearrange("q t h d -> q (t h) d")[:, :, 0:DH], ACT.Square
                               ).then_inc(osq_ready, 1)

            def read_yT(p):
                for n in range(KT):
                    act.wait_ge(yT_done, KT * p + n + 1)
                    if n == 0 and not (isinstance(p, int) and p == 0):
                        act.wait_ge(pu_done, 8 * FT * p)
                    act.activation(yT[:, 0, n], pq[:, n % 2], ACT.Copy).then_inc(yh_ready, 1)

            def ffn_up(q, j):
                for w in range(2):
                    n = 2 * j + w
                    o = j + w * FT
                    if n >= 2:
                        act.wait_ge(acc_ready, 4 * FT * q + 2 * n - 3)
                    for g in range(2):
                        act.wait_ge(pu_done, 8 * FT * q + 4 * n + g + 1)
                        act.activation(ffn[:, 2 * (n % 2) + g], pf[:, g], ACT.Copy,
                                       scale=gu_scale[:, g * GU + o:g * GU + o + 1]).then_inc(t_ready, 1)
                    if w == 1:
                        act.wait_ge(acc_ready, 4 * FT * q + 4 * j + 2)
                        if j >= 2:
                            act.wait_ge(h_ready, FT * q + j - 1)
                        act.activation(th[:, j % 2], ffn[:, 4 + j % 2], ACT.Tanh, scale=0.5
                                       ).then_inc(th_ready, 1)

            def down(q, tt):
                act.wait_ge(dn_done, TT * q + tt + 1)
                if tt == 0:
                    act.wait_ge(h_ready, FT * q + FT)
                if tt > 0:
                    act.wait_ge(ss_ready, TT * q + tt)
                act.activation(th[:, 0], pf[:, tt], ACT.Square, accum_out=ssq[:, tt:tt + 1]
                               ).then_inc(ss_ready, 1)

            def prepare(j):
                if j == 0:
                    act.wait_ge(sc_done, 1)
                    act.activation(gu_scale[:].rearrange("q (g w o) -> q g w o", g=KT, w=2)[:, :, 0],
                                   pf[:, 0].bitcast(F16)[:, 0:KT * GU].rearrange(
                                       "q (g w o) -> q g w o", g=KT, w=2)[:, :, 0],
                                   ACT.Copy, scale=1.0 / PX).then_inc(sc_ready, 1)
                    act.activation(gu_scale[:].rearrange("q (g w o) -> q g w o", g=KT, w=2)[:, :, 1],
                                   pf[:, 0].bitcast(F16)[:, 0:KT * GU].rearrange(
                                       "q (g w o) -> q g w o", g=KT, w=2)[:, :, 1],
                                   ACT.Copy, scale=0.5 / PX).then_inc(sc_ready, 1)
                    act.activation(dn_scale[:], pf[:, 1].bitcast(F16)[:, 0:FT * KT], ACT.Copy,
                                   scale=FP4_SCALE).then_inc(sc_ready, 1)
                for n in {1: range(5), 2: range(5, FT)}.get(j, ()):
                    act.wait_ge(gut_done, n + 1)
                    act.activation(gu_val[:, 2 * n:2 * n + 2].rearrange("q o g k -> q (o g k)"),
                                   pf[:, n % 4].bitcast(F16), ACT.Copy, scale=FP4_SCALE).then_inc(gut_read, 1)
                for n in {5: range(4), 6: range(4, 8), 7: range(8, FT)}.get(j, ()):
                    act.wait_ge(dnt_done, n + 1)
                    act.activation(w_down[:, n], pf[:, n % 4], ACT.Copy).then_inc(dnt_read, 1)

            def iteration(p, q):
                if p is not None:
                    chain.start(p)
                for j in range(FT):
                    if q is not None:
                        ffn_up(q, j)
                    else:
                        prepare(j)
                    if p is not None:
                        if j == 1:
                            read_xT(p)
                        if j == 3:
                            softplus(p)
                        if j == 4:
                            floors(p)
                            exps(p, 0)
                        if j >= 5:
                            if j >= 6:
                                read_o(p, j - 6)
                            exps(p, j - 4)
                if q is not None:
                    down(q, 0)
                if p is not None:
                    read_o(p, 5)
                    exps(p, 7)
                if q is not None:
                    down(q, 1)
                if p is not None:
                    read_o(p, 6)
                if q is not None:
                    down(q, 2)
                if p is not None:
                    read_o(p, 7)
                    squares(p)
                if q is not None:
                    down(q, 3)
                if p is not None:
                    read_yT(p)

            iteration(0, None)
            with act.Fori(1, PAIRS) as p:
                iteration(p, p - 1)
            iteration(None, PAIRS - 1)

        @block.tensor
        def _(pe):
            def turn_x(p):
                for n in range(2 * KT):
                    if n == 0:
                        pe.wait_ge(xn_ready, p + 1)
                        if not (isinstance(p, int) and p == 0):
                            pe.wait_ge(yh_ready, KT * p)
                            pe.wait_ge(yl_ready, KT * p)
                    if n == KT:
                        pe.wait_ge(s_ctx, 16 * p + 16)
                    if n >= 2:
                        pe.wait_ge(xT_read, 2 * KT * p + n - 1)
                    for tt in range(TT):
                        c = slice((n % KT) * P, (n % KT + 1) * P)
                        src = xn[:, tt, c] if n < KT else ctx_sb[:, tt, c]
                        last = pe.transpose(pq[:, n % 2, tt * P:(tt + 1) * P], src, ident[:])
                    last.then_inc(xT_done, 1)

            def gate_sums(p):
                pe.wait_ge(xT_read, 2 * KT * (p + 1))
                if isinstance(p, int) and p == 0:
                    pe.wait_ge(wg_ready, 1)
                else:
                    pe.wait_ge(aT_ready, p)
                    pe.wait_ge(floor_ready, p)
                for tt in range(TT):
                    for k in range(2 * KT):
                        last = pe.matmul(pm[:, tt * 2 * NH:(tt + 1) * 2 * NH],
                                         xT[:, k, tt * P:(tt + 1) * P], w_gate[:, k],
                                         start=(k == 0), stop=(k == 2 * KT - 1))
                last.then_inc(g_done, 1)

            def turn_gates(p):
                pe.wait_ge(g_ready, 2 * p + 2)
                for g in range(2):
                    for c in range(2):
                        last = pe.transpose(pm[0:2 * NH, g * S + c * P:g * S + (c + 1) * P],
                                            g_sb[:, g, c].rearrange("q b h -> q (b h)"), ident[:])
                last.then_inc(gT_done, 1)

            def turn_back(p):
                pe.wait_ge(am_ready, 2 * p + 2)
                take_wait(pe)
                for w in range(2):
                    for c in range(2):
                        k = (2 * w + c) * 2 * NH
                        last = pe.transpose(pm[:, k:k + 2 * NH], am[:, w, c * P:(c + 1) * P],
                                            ident[0:2 * NH, 0:2 * NH])
                last.then_inc(back_done, 1)

            def scores(p, u):
                hg, b = u // 2, u % 2
                pe.wait_ge(qdiag_ready, NH * p + HG * (hg + 1))
                for blk, (t, s) in enumerate(((0, 0), (0, 1), (1, 1))):
                    n = 3 * u + blk
                    if n >= 2:
                        pe.wait_ge(prod_done, 3 * UNITS * p + n - 1)
                    k0, q0 = b * S + t * P, b * S + s * P
                    pe.matmul(pq[:, n % 2], xT[:, KT + hg, k0:k0 + P],
                              q_diag[:, hg % 2, :, q0:q0 + P], start=True, stop=True).then_inc(qk_done, 1)

            def values(p, u):
                hg, b = u // 2, u % 2
                pe.wait_ge(prod_done, 3 * UNITS * p + 3 * u + 3)
                if u == 0:
                    pe.wait_ge(v_ready, TT * p + TT)
                if u > 0:
                    pe.wait_ge(o_read, UNITS * p + u)
                elif not (isinstance(p, int) and p == 0):
                    pe.wait_ge(o_read, UNITS * p)
                for s in range(2):
                    for h in range(HG):
                        o = po[:, (s * HG + h) * (DH + 1):(s * HG + h + 1) * (DH + 1)]
                        head = hg * HG + h
                        for t in range(s + 1):
                            last = pe.matmul(o, dmat[:, u % 2, s + t, h], v_sb[:, 2 * b + t, head],
                                             start=(t == 0), stop=(t == s))
                last.then_inc(pv_done, 1)

            def turn_y(p):
                pe.wait_ge(yn_ready, p + 1)
                for n in range(KT):
                    if n < 2:
                        pe.wait_ge(prod_done, 3 * UNITS * (p + 1))
                    else:
                        pe.wait_ge(yh_ready, KT * p + n - 1)
                        pe.wait_ge(yl_ready, KT * p + n - 1)
                    for tt in range(TT):
                        last = pe.transpose(pq[:, n % 2, tt * P:(tt + 1) * P],
                                            xn[:, tt, n * P:(n + 1) * P], ident[:])
                    last.then_inc(yT_done, 1)

            def ffn_up(q, j):
                if j == 0:
                    pe.wait_ge(yh_ready, KT * q + KT)
                    pe.wait_ge(yl_ready, KT * q + KT)
                for w in range(2):
                    n = 2 * j + w
                    for g in range(KT):
                        if n >= 1:
                            if g < 2:
                                pe.wait_ge(t_ready, 4 * FT * q + 2 * n - 1 + g)
                            else:
                                pe.wait_ge(acc_ready, 4 * FT * q + 2 * n - 3 + g)
                        for part in range(2):
                            last = pe.matmul(pf[:, g], gu_val[:, j + w * FT, g], yT[:, part, g],
                                             start=(part == 0), stop=(part == 1))
                        last.then_inc(pu_done, 1)

            def down(q, tt):
                if tt == 0:
                    pe.wait_ge(h_ready, FT * q + FT)
                    pe.wait_ge(t_ready, 4 * FT * (q + 1))
                if tt == 2:
                    pe.wait_ge(acc_ready, 4 * FT * (q + 1))
                for j in range(FT):
                    last = pe.matmul(pf[:, tt], hT[:, j, tt * P:(tt + 1) * P], w_down[:, j],
                                     start=(j == 0), stop=(j == FT - 1))
                last.then_inc(dn_done, 1)

            def prepare(j):
                if j == 0:
                    pe.wait_ge(const_ready, 6)
                    pe.wait_ge(s_const, 16 * 7)
                    pe.transpose(pf[:, 0].bitcast(F16)[:, 0:KT * GU], sc_raw[:], ident16[0:KT * GU, 0:KT * GU])
                    pe.transpose(pf[:, 1].bitcast(F16)[:, 0:FT * KT], dsc_raw[:],
                                 ident16[0:FT * KT, 0:FT * KT]).then_inc(sc_done, 1)
                for n in {1: range(5), 2: range(5, FT)}.get(j, ()):
                    if n == 0:
                        pe.wait_ge(sc_ready, 3)
                    pe.wait_ge(fp4_ready, 1 if 2 * n + 1 < FT else 2)
                    if n >= 4:
                        pe.wait_ge(gut_read, n - 3)
                    for o in range(2):
                        for g in range(KT):
                            k = (o * KT + g) * P
                            last = pe.transpose(
                                pf[:, n % 4].bitcast(F16)[:, k:k + P],
                                gu_fp4[:, 2 * n + o, g * P:(g + 1) * P],
                                ident16[:])
                    last.then_inc(gut_done, 1)
                for n in {5: range(4), 6: range(4, 8), 7: range(8, FT)}.get(j, ()):
                    if n == 0:
                        pe.wait_ge(dn32_ready, 4 * KT)
                        pe.wait_ge(gut_read, FT)
                    if n >= 4:
                        pe.wait_ge(dnt_read, n - 3)
                    for o in range(KT):
                        last = pe.transpose(
                            pf[:, n % 4, o * P:(o + 1) * P],
                            dn_f32[:, o, n * P:(n + 1) * P],
                            ident[:])
                    last.then_inc(dnt_done, 1)

            def iteration(p, q):
                for j in range(FT):
                    if q is not None:
                        ffn_up(q, j)
                    else:
                        prepare(j)
                    if p is not None:
                        if j == 1:
                            turn_x(p)
                        if j == 2:
                            gate_sums(p)
                        if j == 3:
                            turn_gates(p)
                        if j == 4:
                            turn_back(p)
                        if j >= 5:
                            scores(p, j - 5)
                        if j >= 6:
                            values(p, j - 6)
                if q is not None:
                    down(q, 0)
                if p is not None:
                    scores(p, 6)
                    values(p, 5)
                if q is not None:
                    down(q, 1)
                if p is not None:
                    scores(p, 7)
                    values(p, 6)
                    values(p, 7)
                if q is not None:
                    down(q, 2)
                    down(q, 3)
                if p is not None:
                    turn_y(p)

            iteration(0, None)
            with pe.Fori(1, PAIRS) as p:
                iteration(p, p - 1)
            pe.wait_ge(dnt_read, FT)
            iteration(None, PAIRS - 1)

        @block.vector
        def _(dve):
            chain = Chain(dve, dve_a)
            link = chain.link

            def stats(k, tt):
                link(dve.bn_stats(bst[:, k, tt], x_sb[:, tt]))
                take_wait(dve)
                chain.inc(dve.bn_aggr(mv[:, k, tt], bst[:, k, tt]))

            def norm1(p):
                dve.wait_ge(s_x, 16 * p + 16)
                for tt in range(TT):
                    stats(0, tt)
                chain.wait()
                dve.tensor_scalar(vv[:, 0], mv[:, 0, :, 1], EPS_LN, None, ALU.add).then_inc(var1_ready, 1)
                dve.wait_ge(s_ctx, 16 * p + 16)
                link(dve.tensor_reduce(vmean[:, 0], ctx_sb[:].rearrange("q t (h d) -> q (t h) d", d=DH),
                                       AX.X, ALU.add))
                dve.tensor_scalar(vmean[:, 1], vmean[:, 0], -1.0 / DH, None, ALU.mult).then_inc(vmean_ready, 1)
                dve.wait_ge(rstd1_ready, p + 1)
                if not (isinstance(p, int) and p == 0):
                    dve.wait_ge(yT_done, KT * p)
                for tt in range(TT):
                    last = dve.tensor_scalar(xn[:, tt], x_sb[:, tt], mv[:, 0, tt, 0:1], rs[:, 0, tt:tt + 1],
                                             ALU.subtract, ALU.mult)
                last.then_inc(xn_ready, 1)

            def gate_bias(p):
                dve.wait_ge(g_done, p + 1)
                if isinstance(p, int) and p == 0:
                    dve.wait_ge(s_const, 16 * 7)
                bias = bias_row[:].rearrange("q (g h) -> q g h", g=2)
                for b in range(2):
                    for c in range(2):
                        k = (2 * b + c) * 2 * NH
                        last = dve.tensor_tensor(g_sb[:, :, c, b], pm[:, k:k + 2 * NH].rearrange(
                            "q (g h) -> q g h", g=2), bias, ALU.add)
                    last.then_inc(g_ready, 1)

            def scans(p):
                dve.wait_ge(gT_done, p + 1)
                link(dve.tensor_copy(gates.rearrange("q g s -> q (g s)"), pm[0:2 * NH, :]))
                dve.scalar_tensor_tensor(lf[:, 0], gates[:, 1], -1.0, gates[:, 1], ALU.mult, ALU.max
                                         ).then_inc(absf_ready, 1)
                dve.wait_ge(softp_ready, p + 1)
                link(dve.scalar_tensor_tensor(lf[:, 3], gates[:, 1], 0.0, lf[:, 2], ALU.min, ALU.subtract))
                link(dve.tensor_tensor_scan(lf[:, 1], lf[:, 3], lf[:, 3], 0.0, ALU.add, ALU.min))
                ins = dve.tensor_tensor(am[:, 0], gates[:, 0], lf[:, 1], ALU.subtract)
                ins.then_inc(am_ready, 1)
                dve.wait_ge(am_ready, 2 * p + 1)
                link(dve.tensor_tensor_scan(lf[:, 2], am[:, 0], am[:, 0], -3.0e38, ALU.max, ALU.max))
                if not (isinstance(p, int) and p == 0):
                    dve.wait_ge(s_nm, 16 * p)
                dve.tensor_scalar(nm[:], lf[:, 2], -1.0, None, ALU.mult).then_inc(nm_ready, 1)
                dve.scalar_tensor_tensor(am[:, 1], lf[:, 2], -1.0, lf[:, 1], ALU.mult, ALU.subtract
                                         ).then_inc(am_ready, 1)

            def read_a(p):
                dve.wait_ge(back_done, p + 1)
                if not (isinstance(p, int) and p == 0):
                    dve.wait_ge(exp_done, UNITS * p)
                dve.tensor_copy(aT[:].rearrange("q c n -> q (c n)"), pm[:, 0:4 * NH]).then_inc(aT_ready, 1)

            def products(p, u):
                dve.wait_ge(mask_done, 2 * UNITS * p + 2 * u + 2)
                for blk in range(3):
                    n = 3 * u + blk
                    dve.wait_ge(qk_done, 3 * UNITS * p + n + 1)
                    d = dmat[:, u % 2, blk].rearrange("q h s -> q (h s)")
                    dve.scalar_tensor_tensor(d, pq[:, n % 2], float(DH) ** -0.5, d, ALU.mult, ALU.mult
                                             ).then_inc(prod_done, 1)

            def post(p):
                sums = tok[:].rearrange("q t h d -> q (t h) d")
                dve.wait_ge(o_read, UNITS * p + UNITS)
                dve.wait_ge(floor_ready, p + 1)
                link(dve.scalar_tensor_tensor(hn[:, 0], sums[:, :, DH], -1.0, sums[:, :, DH],
                                              ALU.mult, ALU.max))
                link(dve.tensor_tensor(hn[:, 1], hn[:, 0], floor[:].rearrange("q b c h -> q (b c h)"),
                                       ALU.max))
                link(dve.tensor_scalar(hn[:, 1], hn[:, 1], EPS, None, ALU.add))
                chain.inc(dve.tensor_tensor(hn[:, 2], hn[:, 1], hn[:, 1], ALU.mult))
                dve.wait_ge(osq_ready, p + 1)
                link(dve.tensor_reduce(hn[:, 0], osq, AX.X, ALU.add))
                link(dve.tensor_scalar(hn[:, 1], hn[:, 0], 1.0 / DH, None, ALU.mult))
                dve.scalar_tensor_tensor(hn[:, 3], hn[:, 2], EPS, hn[:, 1], ALU.mult, ALU.add
                                         ).then_inc(hvar_ready, 1)
                dve.wait_ge(hrstd_ready, p + 1)
                for tt in range(TT):
                    dve.wait_ge(ols_ready, TT * p + tt + 1)
                    o = tok[:, tt, :, 0:DH]
                    r = hr[:, tt * NH:(tt + 1) * NH].unsqueeze(2).to_broadcast([P, NH, DH])
                    link(dve.tensor_tensor(o, o, r, ALU.mult))
                    xt = x_sb[:, tt].rearrange("q (h d) -> q h d", d=DH)
                    dve.tensor_tensor(xt, xt, o, ALU.add).then_inc(x1_ready, 1)

            def norm2(p):
                for tt in range(TT):
                    dve.wait_ge(x1_ready, TT * p + tt + 1)
                    stats(1, tt)
                chain.wait()
                dve.tensor_scalar(vv[:, 1], mv[:, 1, :, 1], EPS_LN, None, ALU.add).then_inc(var2_ready, 1)
                dve.wait_ge(rstd2_ready, p + 1)
                link(dve.tensor_scalar(rk[:], rs[:, 1], PX, None, ALU.mult))
                for tt in range(TT):
                    last = dve.tensor_scalar(xn[:, tt].rearrange("q (w i h) -> q w h i", i=4, h=2),
                                             x_sb[:, tt].rearrange("q (w h i) -> q w h i", i=4, h=2),
                                             mv[:, 1, tt, 0:1], rk[:, tt:tt + 1], ALU.subtract, ALU.mult)
                last.then_inc(yn_ready, 1)

            def low_yT(p):
                for n in range(KT):
                    dve.wait_ge(yh_ready, KT * p + n + 1)
                    dve.tensor_tensor(yT[:, 1, n], pq[:, n % 2], yT[:, 0, n], ALU.subtract
                                      ).then_inc(yl_ready, 1)

            def ffn_up(q, j):
                for w in range(2):
                    n = 2 * j + w
                    o = j + w * FT
                    acc = ffn[:, 4 + 2 * w + j % 2]
                    if w == 1 and j >= 2:
                        dve.wait_ge(h_ready, FT * q + j - 1)
                    dve.wait_ge(tsum_ready, 2 * FT * q + n + 1)
                    dve.wait_ge(pu_done, 8 * FT * q + 4 * n + 3)
                    dve.scalar_tensor_tensor(acc, pf[:, 2], gu_scale[:, 2 * GU + o:2 * GU + o + 1],
                                             ffn[:, 2 * (n % 2)], ALU.mult, ALU.add).then_inc(acc_ready, 1)
                    dve.wait_ge(pu_done, 8 * FT * q + 4 * n + 4)
                    dve.wait_ge(acc_ready, 4 * FT * q + 2 * n + 1)
                    dve.scalar_tensor_tensor(acc, pf[:, 3], gu_scale[:, 3 * GU + o:3 * GU + o + 1],
                                             acc, ALU.mult, ALU.add).then_inc(acc_ready, 1)
                dve.wait_ge(th_ready, FT * q + j + 1)
                dve.scalar_tensor_tensor(th[:, j % 2], th[:, j % 2], 1.0, ffn[:, 4 + j % 2],
                                         ALU.add, ALU.mult).then_inc(gg_ready, 1)

            def down(q, half):
                c = slice(2 * half, 2 * half + 2)
                dve.wait_ge(ss_ready, TT * q + 2 * half + 2)
                dve.tensor_scalar(ms[:, c], ssq[:, c], 1.0 / E, EPS, ALU.mult, ALU.add).then_inc(ms_ready, 1)
                dve.wait_ge(yr_ready, 2 * q + half + 1)
                dve.wait_ge(s_res, 16 * q + 16)
                for tt in range(2 * half, 2 * half + 2):
                    dve.scalar_tensor_tensor(x_res[:, tt], pf[:, tt], yr[:, tt:tt + 1], x_res[:, tt],
                                             ALU.mult, ALU.add).then_inc(o_ready, 1)

            own = [0]

            def step(ins):
                ins.then_inc(dve_w, 1)
                own[0] += 1
                dve.wait_ge(dve_w, own[0])

            def decode(words, dst, a, bb):
                for i in range(4):
                    step(dve.tensor_scalar(a, words, 12 - 4 * i, SIGN_MASK, ALU.logical_shift_left,
                                           ALU.bitwise_and))
                    if i < 3:
                        step(dve.tensor_scalar(bb, words, 9 - 4 * i, MAGN_MASK, ALU.logical_shift_left,
                                               ALU.bitwise_and))
                    else:
                        step(dve.tensor_scalar(bb, words, 3, MAGN_MASK, ALU.logical_shift_right,
                                               ALU.bitwise_and))
                    step(dve.tensor_tensor(dst(i), a, bb, ALU.bitwise_or))
                dve.sem_inc(fp4_ready, 1)

            def prepare(j):
                if j == 0:
                    dve.wait_ge(s_const, 16 * 7)
                    dve.tensor_tensor(w_gate[:, KT:2 * KT], w_gate[:, KT:2 * KT], w_gate[:, 2 * KT:3 * KT],
                                      ALU.add).then_inc(wg_ready, 1)
                    dve.wait_ge(s_words, 32)
                if j < 2:
                    o = slice(j * FT, (j + 1) * FT)
                    a, bb = (bits[:, k * FT * NW:(k + 1) * FT * NW].rearrange("q (o w) -> q o w", o=FT)
                             for k in range(2))
                    decode(gu_words[:, o], lambda i: gu_bits[:, o, :, i], a, bb)
                if j == 2:
                    a, bb = (bits[:, k * KT * DW:(k + 1) * KT * DW].rearrange("q (o w) -> q o w", o=KT)
                             for k in range(2))
                    decode(dn_words, lambda i: dn_bits[:, :, :, i], a, bb)
                if j == 3:
                    dve.wait_ge(gut_done, FT)
                    dve.wait_ge(sc_ready, 3)
                    for o in range(KT):
                        for i in range(4):
                            s = dn_scale[:].rearrange("q (g o) -> q g o", o=KT)[:, :, o]
                            dve.tensor_tensor(
                                dn_f32[:, o].rearrange("q (g w h i) -> q i g w h", g=FT, h=2, i=4)[:, i],
                                dn_fp4[:, o, i], s.unsqueeze(2).unsqueeze(3).to_broadcast([P, FT, 16, 2]),
                                ALU.mult).then_inc(dn32_ready, 1)

            def iteration(p, q):
                if p is not None:
                    chain.start(p)
                for j in range(FT):
                    if q is not None:
                        ffn_up(q, j)
                    elif j > 0:
                        prepare(j)
                    if p is not None:
                        if j == 1:
                            norm1(p)
                        if j == 2:
                            gate_bias(p)
                        if j == 3:
                            scans(p)
                        if j == 4:
                            read_a(p)
                        if j >= 5:
                            products(p, j - 5)
                if p is not None:
                    products(p, 6)
                if q is not None:
                    down(q, 0)
                if p is not None:
                    products(p, 7)
                    post(p)
                    norm2(p)
                if q is not None:
                    down(q, 1)
                if p is not None:
                    low_yT(p)

            prepare(0)
            iteration(0, None)
            with dve.Fori(1, PAIRS) as p:
                iteration(p, p - 1)
            iteration(None, PAIRS - 1)


_INS = ["x", "ctx_2048", "L0_xattn_Wi", "L0_xattn_bi", "L0_xattn_Wf", "L0_xattn_bf", "L0_xattn_ln_scale",
        "L0_ffn_gate_up_packed", "L0_ffn_gate_up_scales", "L0_ffn_down_packed", "L0_ffn_down_scales"]


def kernel(**inputs):
    import numpy as _np
    import concourse.bacc as _bacc
    from concourse import mybir as _mybir
    from concourse.bass_utils import run_bass_kernel_spmd as _run

    nc = _bacc.Bacc("TRN2", target_bir_lowering=False, num_devices=1)
    arrays, args = {}, []
    for name in _INS:
        a = _np.ascontiguousarray(inputs[name])
        arrays[f"in_{name}"] = a
        args.append(nc.dram_tensor(f"in_{name}", a.shape, _mybir.dt.from_np(a.dtype), kind="ExternalInput").ap())
    args.append(nc.dram_tensor("out_0", (B, S, E), F32, kind="ExternalOutput").ap())
    xattn_ffn(nc, *args)
    r = _run(nc, [arrays], core_ids=[0])
    return r.results[0]["out_0"]
```

```python
from contextlib import ExitStack

import concourse.bass as bass
from concourse import mybir

F32 = mybir.dt.float32
F16 = mybir.dt.float16
I32 = mybir.dt.int32
ALU = mybir.AluOpType
ACT = mybir.ActivationFunctionType
AX = mybir.AxisListType

P = 128
B, S, E, NH = 8, 256, 512, 16
DH = E // NH
PAIRS = B // 2
TT = 2 * S // P
KT = E // P
HG = P // DH
I = 1408
FT = I // P
GU = 2 * FT
NW = E // 8
DW = I // 8
UNITS = 2 * KT
PX = 1024.0
EPS_LN = 1e-5
EPS = 1e-6
FP4_SCALE = 16384.0
SIGN_MASK = 0x80008000 - (1 << 32)
MAGN_MASK = 0x0E000E00


VAR_MAX = 1e38
RSQRT_START = float(0x5F3759DF)

SCORES_AT = [1, 3, 5, 7, 9, 11, 13, 15]
EXPS = {max(h - 2, 0): u for u, h in enumerate(SCORES_AT)}
SCORES = {h: u for u, h in enumerate(SCORES_AT)}
PRODUCTS = {h + 1: u for u, h in enumerate(SCORES_AT)}
VALUES = PRODUCTS
READ_O = {h + 2: u for u, h in enumerate(SCORES_AT)}
SPREAD = {SCORES_AT[3] + 1: 2, SCORES_AT[5] + 1: 3}


class Chain:

    def __init__(self, eng, sem):
        self.eng, self.sem, self.per, self.n, self.base = eng, sem, None, 0, 0

    def start(self, p):
        if self.per is None and self.n:
            self.per = self.n
        self.base = 0 if self.per is None else p * self.per
        self.n = 0

    def inc(self, ins):
        ins.then_inc(self.sem, 1)
        self.n += 1

    def wait(self):
        self.eng.wait_ge(self.sem, self.base + self.n)

    def link(self, ins):
        self.inc(ins)
        self.wait()


def xattn_ffn(nc, x, ctx, Wi, bi, Wf, bf, ln_scale, gu_packed, gu_scales, dn_packed, dn_scales, out):
    x_pairs = x.rearrange("(p b) (c q) d -> p q (b c) d", b=2, q=P)
    ctx_pairs = ctx.rearrange("(p b) (c q) d -> p q (b c) d", b=2, q=P)
    out_pairs = out.rearrange("(p b) (c q) d -> p q (b c) d", b=2, q=P)
    negm_dram = nc.dram_tensor("negm_dram", (2 * NH, S), F32, kind="Internal").ap()

    es = ExitStack()
    with es:
        def sb(name, shape, dt=F32):
            return es.enter_context(nc.sbuf_tensor(name, shape, dt))

        def sem(name):
            return es.enter_context(nc.semaphore(name))

        ident = sb("ident", [P, P])
        ident16 = sb("ident16", [P, P], F16)
        neghalf = sb("neghalf", [P, TT * NH])
        bias_row = sb("bias_row", [P, 2 * NH])
        ln_row = sb("ln_row", [P, E])
        w_gate = sb("w_gate", [P, 12, 2 * NH])
        gu_val = sb("gu_val", [P, GU, KT, P], F16)
        w_down = sb("w_down", [P, FT, E])
        gu_scale = sb("gu_scale", [P, KT * GU])
        dn_scale = sb("dn_scale", [P, FT * KT])
        sc_raw = sb("sc_raw", [KT * GU, P], F16)
        dsc_raw = sb("dsc_raw", [FT * KT, P], F16)
        x_sb = sb("x_sb", [P, TT, E])
        x_res = sb("x_res", [P, TT, E])
        ctx_sb = sb("ctx_sb", [P, TT, E])
        tok = sb("tok", [P, TT, NH, DH + 1])
        xT = sb("xT", [P, 2 * KT, TT * P])
        v_sb = sb("v_sb", [P, TT, NH, DH + 1])
        q_diag = sb("q_diag", [P, 2, HG, TT * P])
        negm = sb("negm", [P, 4, HG, S])
        dmat = sb("dmat", [P, 2, 3, HG, P])
        yT = sb("yT", [P, 2, KT, TT * P], F16)
        ffn = sb("ffn", [P, 8, TT * P])
        th = sb("th", [P, 2, TT * P])
        hT = sb("hT", [P, FT, TT * P])
        g_sb = sb("g_sb", [P, 2, 2, 2, NH])
        gates = negm[0:2 * NH, 2, 0:2]
        lf = negm[0:2 * NH, 3]
        am = sb("am", [2 * NH, 2, S])
        nm = sb("nm", [2 * NH, S])
        aT = sb("aT", [P, 2, 2 * NH])
        floor = sb("floor", [P, 2, 2, NH])
        bst = sb("bst", [P, 2, TT, 6])
        mv = sb("mv", [P, 2, TT, 2])
        vv = sb("vv", [P, 2, TT])
        rs = sb("rs", [P, 2, TT])
        rk = sb("rk", [P, TT])
        vmean = sb("vmean", [P, 2, TT * NH])
        hn = sb("hn", [P, 4, TT * NH])
        hr = sb("hr", [P, TT * NH])
        ssq = sb("ssq", [P, TT])
        ms = sb("ms", [P, TT])
        yr = sb("yr", [P, TT])
        gu_words = x_res[:].rearrange("p a b -> p (a b)").bitcast(I32)[:, 0:GU * NW].rearrange(
            "p (o w) -> p o w", o=GU)
        dn_words = th[:].rearrange("p a b -> p (a b)").bitcast(I32)[:, 0:KT * DW].rearrange(
            "p (o w) -> p o w", o=KT)
        bits = yT[:].rearrange("p a b c -> p (a b c)").bitcast(I32)
        gu_bits = hT[:].rearrange("p a b -> p (a b)").bitcast(I32).rearrange(
            "p (o w i) -> p o w i", o=GU, i=4)
        gu_fp4 = hT[:].rearrange("p a b -> p (a b)").bitcast(F16).rearrange(
            "p (o k) -> p o k", o=GU)
        dn_bits = ffn[:].rearrange("p a b -> p (a b)").bitcast(I32)[:, 0:KT * 4 * DW].rearrange(
            "p (o w i) -> p o w i", o=KT, i=4)
        dn_fp4 = ffn[:].rearrange("p a b -> p (a b)").bitcast(F16)[:, 0:KT * I].rearrange(
            "p (o g w i h) -> p o i g w h", o=KT, g=FT, i=4, h=2)
        dn_f32 = hT[:].rearrange("p a b -> p (a b)").rearrange("p (o k) -> p o k", o=KT)
        xg = ffn[:, 0:TT]
        yn = tok[:].rearrange("p a b c -> p a (b c)")[:, :, 0:E]
        osq = dmat[:].rearrange("p a b c d -> p (a b c d)")[:, 0:TT * E].rearrange(
            "p (g d) -> p g d", d=DH)

        pf = es.enter_context(nc.psum_tensor("pf", [P, 4, 512], F32))
        pq = es.enter_context(nc.psum_tensor("pq", [P, 3, 512], F32))
        po = es.enter_context(nc.psum_tensor("po", [P, 512], F32))
        pm = pq[:, 2]

        s_const = sem("s_const")
        s_words = sem("s_words")
        s_x = sem("s_x")
        s_xg = sem("s_xg")
        s_ctx = sem("s_ctx")
        s_res = sem("s_res")
        s_nm = sem("s_nm")
        s_negm = [sem(f"s_negm{i}") for i in range(4)]
        s_out = sem("s_out")
        const_ready = sem("const_ready")
        wg_ready = sem("wg_ready")
        sc_done = sem("sc_done")
        sc_ready = sem("sc_ready")
        fp4_ready = sem("fp4_ready")
        gut_done = sem("gut_done")
        gut_read = sem("gut_read")
        dn32_ready = sem("dn32_ready")
        dnt_done = sem("dnt_done")
        dnt_read = sem("dnt_read")
        waits_taken = sem("waits_taken")
        dve_w = sem("dve_w")
        dve_g1 = sem("dve_g1")
        dve_g2 = sem("dve_g2")
        dve_p = sem("dve_p")
        act_g = sem("act_g")
        var1_ready = sem("var1_ready")
        rstd1_ready = sem("rstd1_ready")
        xn_ready = sem("xn_ready")
        vmean_ready = sem("vmean_ready")
        v_ready = sem("v_ready")
        xT_done = sem("xT_done")
        xT_read = sem("xT_read")
        g_done = sem("g_done")
        g_ready = sem("g_ready")
        gT_done = sem("gT_done")
        absf_ready = sem("absf_ready")
        softp_ready = sem("softp_ready")
        nm_ready = sem("nm_ready")
        am_ready = sem("am_ready")
        back_done = sem("back_done")
        aT_ready = sem("aT_ready")
        floor_ready = sem("floor_ready")
        qdiag_ready = sem("qdiag_ready")
        qk_done = sem("qk_done")
        exp_done = sem("exp_done")
        mask_done = sem("mask_done")
        prod_done = sem("prod_done")
        pv_done = sem("pv_done")
        o_read = sem("o_read")
        osq_ready = sem("osq_ready")
        oscaled = sem("oscaled")
        hvar_ready = sem("hvar_ready")
        ols_ready = sem("ols_ready")
        x1_ready = sem("x1_ready")
        var2_ready = sem("var2_ready")
        rstd2_ready = sem("rstd2_ready")
        yn_ready = sem("yn_ready")
        yT_done = sem("yT_done")
        yh_ready = sem("yh_ready")
        yl_ready = sem("yl_ready")
        pu_done = sem("pu_done")
        t_ready = sem("t_ready")
        tsum_ready = sem("tsum_ready")
        acc_ready = sem("acc_ready")
        th_ready = sem("th_ready")
        gg_ready = sem("gg_ready")
        h_ready = sem("h_ready")
        dn_done = sem("dn_done")
        ss_ready = sem("ss_ready")
        ms_ready = sem("ms_ready")
        yr_ready = sem("yr_ready")
        o_ready = sem("o_ready")

        def take_wait(eng):
            eng.sem_inc(waits_taken, 1)

        block = es.enter_context(nc.Block())

        @block.sync
        def _(sp):
            def load_ctx(p):
                if not (isinstance(p, int) and p == 0):
                    sp.wait_ge(xT_done, 2 * KT * p)
                    take_wait(sp)
                    sp.wait_ge(v_ready, TT * p)
                sp.dma_start(ctx_sb[:], ctx_pairs[p]).then_inc(s_ctx, 16)

            def load_xg(p, q):
                if q is not None:
                    sp.wait_ge(acc_ready, 4 * FT * q + 4 * FT)
                elif p > 0:
                    sp.wait_ge(dn32_ready, 4 * KT)
                sp.dma_start(xg, x_pairs[p]).then_inc(s_xg, 16)

            def load_x(p):
                sp.dma_start(x_sb[:], x_pairs[p]).then_inc(s_x, 16)

            def keep_residual(q):
                sp.wait_ge(yn_ready, q + 1)
                take_wait(sp)
                sp.wait_ge(x1_ready, 4 * q + 4)
                take_wait(sp)
                sp.dma_start(x_res[:], x_sb[:]).then_inc(s_res, 16)
                sp.wait_ge(s_res, 16 * q + 16)
                take_wait(sp)

            def spread_negm(p):
                sp.wait_ge(nm_ready, p + 1)
                take_wait(sp)
                sp.wait_ge(am_ready, 2 * p + 2)
                take_wait(sp)
                if not (isinstance(p, int) and p == 0):
                    sp.wait_ge(exp_done, UNITS * p)
                sp.dma_start(negm_dram, nm[:]).then_inc(s_nm, 16)
                sp.wait_ge(s_nm, 16 * p + 16)
                take_wait(sp)
                load_units(range(4))

            def late_negm(p):
                for u in range(4, UNITS):
                    sp.wait_ge(exp_done, UNITS * p + u - 3)
                    load_units((u,))

            def load_units(units):
                for u in units:
                    hg, b = u // 2, u % 2
                    r = b * NH + hg * HG
                    sp.dma_start(negm[:, u % 4].rearrange("q h s -> q (h s)"),
                                 negm_dram[r:r + HG, :].rearrange("h s -> (h s)").partition_broadcast(P)
                                 ).then_inc(s_negm[u % 4], 16)

            def store(q, tiles):
                for tt in tiles:
                    sp.wait_ge(o_ready, TT * (q + 1) + tt + 1)
                    sp.dma_start(out_pairs[q][:, tt], x_res[:, tt]).then_inc(s_out, 16)
                if tt == TT - 1:
                    sp.wait_ge(s_out, 16 * TT * q + 16 * TT)
                    take_wait(sp)

            def iteration(p, q, n):
                if q is not None:
                    keep_residual(q)
                if p is not None:
                    load_x(p)
                    if n is not None:
                        load_ctx(n)
                    late_negm(p)
                if n is not None:
                    load_xg(n, q)
                if q is not None:
                    store(q, range(2))
                if n is not None:
                    spread_negm(n)
                if q is not None:
                    store(q, range(2, TT))

            load_xg(0, None)
            load_ctx(0)
            for i, w in enumerate((Wi, Wf)):
                sp.dma_start(w_gate[:, :, i * NH:(i + 1) * NH], w.rearrange("(k q) h -> q k h", q=P)
                             ).then_inc(s_const, 16)
            for i, v in enumerate((bi, bf)):
                sp.dma_start(bias_row[:, i * NH:(i + 1) * NH], v.partition_broadcast(P)
                             ).then_inc(s_const, 16)
            sp.dma_start(ln_row[:], ln_scale.partition_broadcast(P)).then_inc(s_const, 16)
            sp.dma_start(sc_raw[:], gu_scales.rearrange("g (o q) -> (g o) q", q=P)).then_inc(s_const, 16)
            sp.dma_start(dsc_raw[:], dn_scales.rearrange("g (o q) -> (g o) q", q=P)).then_inc(s_const, 16)
            sp.dma_start(gu_words, gu_packed.rearrange("(o q) w -> q o w", q=P)).then_inc(s_words, 16)
            sp.dma_start(dn_words, dn_packed.rearrange("(o q) w -> q o w", q=P)).then_inc(s_words, 16)
            spread_negm(0)
            iteration(0, None, 1)
            sp.wait_ge(fp4_ready, 3)
            with sp.Fori(1, PAIRS - 1) as p:
                iteration(p, p - 1, p + 1)
            iteration(PAIRS - 1, PAIRS - 2, None)
            iteration(None, PAIRS - 1, None)

        @block.gpsimd
        def _(pool):
            def setup():
                pool.memset(ident[:], 0.0).then_inc(const_ready, 1)
                pool.wait_ge(const_ready, 1)
                pool.affine_select(out=ident[:], in_=ident[:], compare_op=ALU.not_equal, fill=1.0, base=0,
                                   pattern=[[-1, P]], channel_multiplier=1).then_inc(const_ready, 1)
                pool.wait_ge(const_ready, 2)
                pool.tensor_copy(ident16[:], ident[:]).then_inc(const_ready, 1)
                pool.memset(neghalf[:], -0.5).then_inc(const_ready, 1)
                pool.memset(v_sb[:, :, :, DH:DH + 1], 1.0).then_inc(const_ready, 1)
                pool.memset(q_diag[:], 0.0).then_inc(const_ready, 1)
                pool.wait_ge(const_ready, 6)

            def rstd1(p):
                pool.wait_ge(var1_ready, p + 1)
                pool.tensor_tensor(rs[:, 0], vv[:, 0], neghalf[:, 0:TT], ALU.pow).then_inc(rstd1_ready, 1)

            def centre_v(p):
                pool.wait_ge(vmean_ready, p + 1)
                pool.wait_ge(s_ctx, 16 * p + 16)
                if not (isinstance(p, int) and p == 0):
                    pool.wait_ge(pv_done, UNITS * p)
                for tt in range(TT):
                    m = vmean[:, 1, tt * NH:(tt + 1) * NH].unsqueeze(2).to_broadcast([P, NH, DH])
                    pool.tensor_tensor(v_sb[:, tt, :, 0:DH],
                                       ctx_sb[:, tt].rearrange("q (h d) -> q h d", d=DH), m, ALU.add
                                       ).then_inc(v_ready, 1)

            def mask(p, u):
                pool.wait_ge(exp_done, UNITS * p + u + 1)
                take_wait(pool)
                for blk in (0, 2):
                    d = dmat[:, u % 2, blk]
                    pool.affine_select(out=d, in_=d, compare_op=ALU.is_ge, fill=0.0, base=0,
                                       pattern=[[0, HG], [1, P]], channel_multiplier=-1
                                       ).then_inc(mask_done, 1)

            def post(p):
                pool.wait_ge(o_read, UNITS * p + UNITS)
                pool.wait_ge(osq_ready, p + 1)
                if isinstance(p, int) and p == 0:
                    pool.wait_ge(s_const, 16 * 7)
                for tt in range(TT):
                    o = tok[:, tt, :, 0:DH]
                    pool.tensor_tensor(o, o, ln_row[:].rearrange("q (h d) -> q h d", d=DH), ALU.mult
                                       ).then_inc(ols_ready, 1)

            def norm2(p):
                pool.wait_ge(var2_ready, p + 1)
                pool.tensor_tensor(rs[:, 1], vv[:, 1], neghalf[:, 0:TT], ALU.pow).then_inc(rstd2_ready, 1)

            def sum_t(q, h):
                pool.wait_ge(t_ready, 4 * FT * q + 2 * h + 2)
                t = ffn[:, 2 * (h % 2)]
                pool.tensor_tensor(t, t, ffn[:, 2 * (h % 2) + 1], ALU.add).then_inc(tsum_ready, 1)

            def gated(q, j):
                pool.wait_ge(acc_ready, 4 * FT * q + 4 * j + 4)
                pool.wait_ge(gg_ready, FT * q + j + 1)
                pool.tensor_tensor(hT[:, j], ffn[:, 6 + j % 2], th[:, j % 2], ALU.mult
                                   ).then_inc(h_ready, 1)

            def down(q, half):
                pool.wait_ge(ms_ready, 2 * q + half + 1)
                c = slice(2 * half, 2 * half + 2)
                pool.tensor_tensor(yr[:, c], ms[:, c], neghalf[:, c], ALU.pow).then_inc(yr_ready, 1)

            def iteration(p, q, n):
                for h in range(GU):
                    if q is not None:
                        sum_t(q, h)
                        if h % 2 == 0 and h > 0:
                            gated(q, h // 2 - 1)
                    if p is not None and h in EXPS:
                        mask(p, EXPS[h])
                if q is not None:
                    gated(q, FT - 1)
                if p is not None:
                    post(p)
                    norm2(p)
                if n is not None:
                    rstd1(n)
                if q is not None:
                    down(q, 0)
                if n is not None:
                    centre_v(n)
                if q is not None:
                    down(q, 1)

            setup()
            rstd1(0)
            centre_v(0)
            iteration(0, None, 1)
            with pool.Fori(1, PAIRS - 1) as p:
                iteration(p, p - 1, p + 1)
            iteration(PAIRS - 1, PAIRS - 2, None)
            iteration(None, PAIRS - 1, None)

        @block.scalar
        def _(act):
            chain = Chain(act, act_g)

            def read_xT(p):
                for n in range(2 * KT):
                    act.wait_ge(xT_done, 2 * KT * p + n + 1)
                    if n == 0 and not (isinstance(p, int) and p == 0):
                        act.wait_ge(qdiag_ready, NH * p)
                        act.wait_ge(qk_done, 3 * UNITS * p)
                    act.activation(xT[:, n], pq[:, n % 2], ACT.Copy).then_inc(xT_read, 1)

            def softplus(p):
                chain.start(p)
                act.wait_ge(absf_ready, p + 1)
                chain.link(act.activation(lf[:, 1], lf[:, 0], ACT.Exp, scale=-1.0))
                act.activation(lf[:, 2], lf[:, 1], ACT.Ln, bias=1.0).then_inc(softp_ready, 1)

            def floors(p):
                act.wait_ge(aT_ready, p + 1)
                if not (isinstance(p, int) and p == 0):
                    act.wait_ge(hvar_ready, p)
                act.activation(floor[:].rearrange("q b c h -> q c b h"),
                               pm[:, 4 * NH:8 * NH].rearrange("q (c b h) -> q c b h", c=2, b=2),
                               ACT.Exp).then_inc(floor_ready, 1)

            def exps(p, u):
                hg, b = u // 2, u % 2
                act.wait_ge(s_negm[u % 4], 32 * p + 16 * (u // 4) + 16)
                act.wait_ge(aT_ready, p + 1)
                if u >= 2:
                    act.wait_ge(pv_done, UNITS * p + u - 1)
                elif not (isinstance(p, int) and p == 0):
                    act.wait_ge(hvar_ready, p)
                for h in range(HG):
                    bh = b * NH + hg * HG + h
                    act.activation(dmat[:, u % 2, 0:2, h],
                                   negm[:, u % 4, h].rearrange("q (c s) -> q c s", c=2), ACT.Exp,
                                   bias=aT[:, 0, bh:bh + 1])
                    last = act.activation(dmat[:, u % 2, 2, h], negm[:, u % 4, h, P:S], ACT.Exp,
                                          bias=aT[:, 1, bh:bh + 1])
                last.then_inc(exp_done, 1)

            def read_o(p, u):
                hg, b = u // 2, u % 2
                act.wait_ge(pv_done, UNITS * p + u + 1)
                act.activation(tok[:, 2 * b:2 * b + 2, hg * HG:(hg + 1) * HG, :].rearrange(
                                   "q c h d -> q c (h d)"),
                               po[:, 0:2 * HG * (DH + 1)].rearrange("q (c n) -> q c n", c=2),
                               ACT.Copy).then_inc(o_read, 1)

            def squares(p):
                act.wait_ge(o_read, UNITS * p + UNITS)
                act.wait_ge(pv_done, UNITS * p + UNITS)
                act.activation(osq, tok[:].rearrange("q t h d -> q (t h) d")[:, :, 0:DH], ACT.Square
                               ).then_inc(osq_ready, 1)

            def read_yT(p):
                for n in range(KT):
                    act.wait_ge(yT_done, KT * p + n + 1)
                    if n == 0 and not (isinstance(p, int) and p == 0):
                        act.wait_ge(pu_done, 8 * FT * p)
                    act.activation(yT[:, 0, n], pq[:, n % 2], ACT.Copy).then_inc(yh_ready, 1)

            def scale_t(q, h):
                o = h // 2 + h % 2 * FT
                if h >= 2:
                    act.wait_ge(acc_ready, 4 * FT * q + 2 * h - 3)
                for g in range(2):
                    act.wait_ge(pu_done, 8 * FT * q + 4 * h + g + 1)
                    act.activation(ffn[:, 2 * (h % 2) + g], pf[:, g], ACT.Copy,
                                   scale=gu_scale[:, g * GU + o:g * GU + o + 1]).then_inc(t_ready, 1)

            def tanh(q, j):
                act.wait_ge(acc_ready, 4 * FT * q + 4 * j + 2)
                if j >= 2:
                    act.wait_ge(h_ready, FT * q + j - 1)
                act.activation(th[:, j % 2], ffn[:, 4 + j % 2], ACT.Tanh, scale=0.5).then_inc(th_ready, 1)

            def down(q, tt):
                act.wait_ge(dn_done, TT * q + tt + 1)
                if tt == 0:
                    act.wait_ge(h_ready, FT * q + FT)
                if tt > 0:
                    act.wait_ge(ss_ready, TT * q + tt)
                act.activation(th[:, 0], pf[:, tt], ACT.Square, accum_out=ssq[:, tt:tt + 1]
                               ).then_inc(ss_ready, 1)

            def prepare(j):
                if j == 0:
                    act.wait_ge(sc_done, 1)
                    act.activation(gu_scale[:].rearrange("q (g w o) -> q g w o", g=KT, w=2)[:, :, 0],
                                   pf[:, 0].bitcast(F16)[:, 0:KT * GU].rearrange(
                                       "q (g w o) -> q g w o", g=KT, w=2)[:, :, 0],
                                   ACT.Copy, scale=1.0 / PX).then_inc(sc_ready, 1)
                    act.activation(gu_scale[:].rearrange("q (g w o) -> q g w o", g=KT, w=2)[:, :, 1],
                                   pf[:, 0].bitcast(F16)[:, 0:KT * GU].rearrange(
                                       "q (g w o) -> q g w o", g=KT, w=2)[:, :, 1],
                                   ACT.Copy, scale=0.5 / PX).then_inc(sc_ready, 1)
                    act.activation(dn_scale[:], pf[:, 1].bitcast(F16)[:, 0:FT * KT], ACT.Copy,
                                   scale=FP4_SCALE).then_inc(sc_ready, 1)
                for n in {1: range(5), 2: range(5, FT)}.get(j, ()):
                    act.wait_ge(gut_done, n + 1)
                    act.activation(gu_val[:, 2 * n:2 * n + 2].rearrange("q o g k -> q (o g k)"),
                                   pf[:, n % 4].bitcast(F16), ACT.Copy, scale=FP4_SCALE).then_inc(gut_read, 1)
                for n in {5: range(4), 6: range(4, 8), 7: range(8, FT)}.get(j, ()):
                    act.wait_ge(dnt_done, n + 1)
                    act.activation(w_down[:, n], pf[:, n % 4], ACT.Copy).then_inc(dnt_read, 1)

            def iteration(p, q, n):
                for h in range(GU):
                    if q is not None:
                        scale_t(q, h)
                    elif h % 2 == 0:
                        prepare(h // 2)
                    if p is not None and h in READ_O:
                        read_o(p, READ_O[h])
                    if q is not None and h % 2:
                        tanh(q, h // 2)
                    if p is not None:
                        if h in EXPS:
                            exps(p, EXPS[h])
                        if h == 1 + max(READ_O):
                            squares(p)
                if q is not None:
                    down(q, 0)
                    down(q, 1)
                if p is not None:
                    read_yT(p)
                if q is not None:
                    down(q, 2)
                if n is not None:
                    read_xT(n)
                if n is not None:
                    softplus(n)
                if q is not None:
                    down(q, 3)
                if n is not None:
                    floors(n)

            read_xT(0)
            softplus(0)
            floors(0)
            iteration(0, None, 1)
            with act.Fori(1, PAIRS - 1) as p:
                iteration(p, p - 1, p + 1)
            iteration(PAIRS - 1, PAIRS - 2, None)
            iteration(None, PAIRS - 1, None)

        @block.tensor
        def _(pe):
            def turn_x(p):
                for n in range(2 * KT):
                    if n == 0:
                        pe.wait_ge(xn_ready, p + 1)
                        if not (isinstance(p, int) and p == 0):
                            pe.wait_ge(yh_ready, KT * p)
                            pe.wait_ge(yl_ready, KT * p)
                    if n == KT:
                        pe.wait_ge(s_ctx, 16 * p + 16)
                    if n >= 2:
                        pe.wait_ge(xT_read, 2 * KT * p + n - 1)
                    for tt in range(TT):
                        c = slice((n % KT) * P, (n % KT + 1) * P)
                        src = xg[:, tt, c] if n < KT else ctx_sb[:, tt, c]
                        last = pe.transpose(pq[:, n % 2, tt * P:(tt + 1) * P], src, ident[:])
                    last.then_inc(xT_done, 1)

            def gate_sums(p):
                pe.wait_ge(xT_read, 2 * KT * (p + 1))
                if isinstance(p, int) and p == 0:
                    pe.wait_ge(wg_ready, 1)
                for tt in range(TT):
                    for k in range(2 * KT):
                        last = pe.matmul(pm[:, tt * 2 * NH:(tt + 1) * 2 * NH],
                                         xT[:, k, tt * P:(tt + 1) * P], w_gate[:, k],
                                         start=(k == 0), stop=(k == 2 * KT - 1))
                last.then_inc(g_done, 1)

            def turn_gates(p):
                pe.wait_ge(g_ready, 2 * p + 2)
                for g in range(2):
                    for c in range(2):
                        last = pe.transpose(pm[0:2 * NH, g * S + c * P:g * S + (c + 1) * P],
                                            g_sb[:, g, c].rearrange("q b h -> q (b h)"), ident[:])
                last.then_inc(gT_done, 1)

            def turn_back(p):
                pe.wait_ge(am_ready, 2 * p + 2)
                take_wait(pe)
                for w in range(2):
                    for c in range(2):
                        k = (2 * w + c) * 2 * NH
                        last = pe.transpose(pm[:, k:k + 2 * NH], am[:, w, c * P:(c + 1) * P],
                                            ident[0:2 * NH, 0:2 * NH])
                last.then_inc(back_done, 1)

            def scores(p, u):
                hg, b = u // 2, u % 2
                pe.wait_ge(qdiag_ready, NH * p + HG * (hg + 1))
                if u == 0:
                    pe.wait_ge(floor_ready, p + 1)
                for blk, (t, s) in enumerate(((0, 0), (0, 1), (1, 1))):
                    if u > 0:
                        pe.wait_ge(prod_done, 3 * UNITS * p + 3 * u - 2 + blk)
                    k0, q0 = b * S + t * P, b * S + s * P
                    pe.matmul(pq[:, blk], xT[:, KT + hg, k0:k0 + P],
                              q_diag[:, hg % 2, :, q0:q0 + P], start=True, stop=True).then_inc(qk_done, 1)

            def values(p, u):
                hg, b = u // 2, u % 2
                pe.wait_ge(prod_done, 3 * UNITS * p + 3 * u + 3)
                if u == 0:
                    pe.wait_ge(v_ready, TT * p + TT)
                if u > 0:
                    pe.wait_ge(o_read, UNITS * p + u)
                elif not (isinstance(p, int) and p == 0):
                    pe.wait_ge(o_read, UNITS * p)
                for s in range(2):
                    for h in range(HG):
                        o = po[:, (s * HG + h) * (DH + 1):(s * HG + h + 1) * (DH + 1)]
                        head = hg * HG + h
                        for t in range(s + 1):
                            last = pe.matmul(o, dmat[:, u % 2, s + t, h], v_sb[:, 2 * b + t, head],
                                             start=(t == 0), stop=(t == s))
                last.then_inc(pv_done, 1)

            def turn_y(p):
                pe.wait_ge(yn_ready, p + 1)
                for n in range(KT):
                    if n < 2:
                        pe.wait_ge(prod_done, 3 * UNITS * (p + 1))
                    else:
                        pe.wait_ge(yh_ready, KT * p + n - 1)
                        pe.wait_ge(yl_ready, KT * p + n - 1)
                    for tt in range(TT):
                        last = pe.transpose(pq[:, n % 2, tt * P:(tt + 1) * P],
                                            yn[:, tt, n * P:(n + 1) * P], ident[:])
                    last.then_inc(yT_done, 1)

            def ffn_up(q, h):
                if h == 0:
                    pe.wait_ge(yh_ready, KT * q + KT)
                    pe.wait_ge(yl_ready, KT * q + KT)
                for g in range(KT):
                    if h >= 1:
                        if g < 2:
                            pe.wait_ge(t_ready, 4 * FT * q + 2 * h - 1 + g)
                        else:
                            pe.wait_ge(acc_ready, 4 * FT * q + 2 * h - 3 + g)
                    else:
                        pe.wait_ge(o_ready, TT * q + g + 1)
                    for part in range(2):
                        last = pe.matmul(pf[:, g], gu_val[:, h // 2 + h % 2 * FT, g], yT[:, part, g],
                                         start=(part == 0), stop=(part == 1))
                    last.then_inc(pu_done, 1)

            def down(q, tt, js):
                if tt == 0 and js[0] == 0:
                    pe.wait_ge(t_ready, 4 * FT * (q + 1))
                if tt == 2 and js[0] == 0:
                    pe.wait_ge(acc_ready, 4 * FT * (q + 1))
                for j in js:
                    if tt == 0:
                        pe.wait_ge(h_ready, FT * q + j + 1)
                    last = pe.matmul(pf[:, tt], hT[:, j, tt * P:(tt + 1) * P], w_down[:, j],
                                     start=(j == 0), stop=(j == FT - 1))
                if js[-1] == FT - 1:
                    last.then_inc(dn_done, 1)

            def prepare(j):
                if j == 0:
                    pe.wait_ge(const_ready, 6)
                    pe.wait_ge(s_const, 16 * 7)
                    pe.transpose(pf[:, 0].bitcast(F16)[:, 0:KT * GU], sc_raw[:], ident16[0:KT * GU, 0:KT * GU])
                    pe.transpose(pf[:, 1].bitcast(F16)[:, 0:FT * KT], dsc_raw[:],
                                 ident16[0:FT * KT, 0:FT * KT]).then_inc(sc_done, 1)
                for n in {1: range(5), 2: range(5, FT)}.get(j, ()):
                    if n == 0:
                        pe.wait_ge(sc_ready, 3)
                    pe.wait_ge(fp4_ready, 1 if 2 * n + 1 < FT else 2)
                    if n >= 4:
                        pe.wait_ge(gut_read, n - 3)
                    for o in range(2):
                        for g in range(KT):
                            k = (o * KT + g) * P
                            last = pe.transpose(
                                pf[:, n % 4].bitcast(F16)[:, k:k + P],
                                gu_fp4[:, 2 * n + o, g * P:(g + 1) * P],
                                ident16[:])
                    last.then_inc(gut_done, 1)
                for n in {5: range(4), 6: range(4, 8), 7: range(8, FT)}.get(j, ()):
                    if n == 0:
                        pe.wait_ge(dn32_ready, 4 * KT)
                        pe.wait_ge(gut_read, FT)
                    if n >= 4:
                        pe.wait_ge(dnt_read, n - 3)
                    for o in range(KT):
                        last = pe.transpose(
                            pf[:, n % 4, o * P:(o + 1) * P],
                            dn_f32[:, o, n * P:(n + 1) * P],
                            ident[:])
                    last.then_inc(dnt_done, 1)

            def iteration(p, q, n):
                for h in range(GU):
                    if q is not None:
                        ffn_up(q, h)
                    elif h % 2 == 0:
                        prepare(h // 2)
                    if p is not None:
                        if h in VALUES:
                            values(p, VALUES[h])
                        if h in SCORES:
                            scores(p, SCORES[h])
                if q is not None:
                    down(q, 0, range(FT))
                    down(q, 1, range(FT))
                if p is not None:
                    turn_y(p)
                if q is not None:
                    down(q, 2, range(FT))
                if n is not None:
                    turn_x(n)
                    gate_sums(n)
                if q is not None:
                    down(q, 3, range(3))
                if n is not None:
                    turn_gates(n)
                if q is not None:
                    down(q, 3, range(3, FT))
                if n is not None:
                    turn_back(n)

            pe.wait_ge(const_ready, 6)
            turn_x(0)
            gate_sums(0)
            turn_gates(0)
            turn_back(0)
            iteration(0, None, 1)
            pe.wait_ge(dnt_read, FT)
            with pe.Fori(1, PAIRS - 1) as p:
                iteration(p, p - 1, p + 1)
            iteration(PAIRS - 1, PAIRS - 2, None)
            iteration(None, PAIRS - 1, None)

        @block.vector
        def _(dve):
            g1, g2, po_steps = Chain(dve, dve_g1), Chain(dve, dve_g2), Chain(dve, dve_p)

            def stats(chain, src, k, tt):
                chain.link(dve.bn_stats(bst[:, k, tt], src))
                take_wait(dve)
                chain.inc(dve.bn_aggr(mv[:, k, tt], bst[:, k, tt]))

            def norm1(p):
                g1.start(p)
                dve.wait_ge(s_xg, 16 * p + 16)
                for tt in range(TT):
                    stats(g1, xg[:, tt], 0, tt)
                g1.wait()
                dve.tensor_scalar(vv[:, 0], mv[:, 0, :, 1], EPS_LN, None, ALU.add).then_inc(var1_ready, 1)
                dve.wait_ge(s_ctx, 16 * p + 16)
                g1.link(dve.tensor_reduce(vmean[:, 0], ctx_sb[:].rearrange("q t (h d) -> q (t h) d", d=DH),
                                       AX.X, ALU.add))
                dve.tensor_scalar(vmean[:, 1], vmean[:, 0], -1.0 / DH, None, ALU.mult).then_inc(vmean_ready, 1)
                dve.wait_ge(rstd1_ready, p + 1)
                for tt in range(TT):
                    last = dve.tensor_scalar(xg[:, tt], xg[:, tt], mv[:, 0, tt, 0:1], rs[:, 0, tt:tt + 1],
                                             ALU.subtract, ALU.mult)
                last.then_inc(xn_ready, 1)

            def spread_q(p, hg):
                dve.wait_ge(xT_read, 2 * KT * p + hg + 1)
                if isinstance(p, int) and p == 0 and hg == 0:
                    dve.wait_ge(const_ready, 6)
                if hg >= 2:
                    dve.wait_ge(qk_done, 3 * UNITS * p + 6 * (hg - 1))
                for h in range(HG):
                    r = slice(h * DH, (h + 1) * DH)
                    dve.tensor_copy(q_diag[r, hg % 2, h], xT[r, hg]).then_inc(qdiag_ready, 1)

            def gate_bias(p):
                dve.wait_ge(g_done, p + 1)
                if isinstance(p, int) and p == 0:
                    dve.wait_ge(s_const, 16 * 7)
                bias = bias_row[:].rearrange("q (g h) -> q g h", g=2)
                for b in range(2):
                    for c in range(2):
                        k = (2 * b + c) * 2 * NH
                        last = dve.tensor_tensor(g_sb[:, :, c, b], pm[:, k:k + 2 * NH].rearrange(
                            "q (g h) -> q g h", g=2), bias, ALU.add)
                    last.then_inc(g_ready, 1)

            def abs_f(p):
                dve.wait_ge(gT_done, p + 1)
                g1.link(dve.tensor_copy(gates.rearrange("q g s -> q (g s)"), pm[0:2 * NH, :]))
                dve.scalar_tensor_tensor(lf[:, 0], gates[:, 1], -1.0, gates[:, 1], ALU.mult, ALU.max
                                         ).then_inc(absf_ready, 1)

            def scans(p):
                g2.start(p)
                dve.wait_ge(softp_ready, p + 1)
                g2.link(dve.scalar_tensor_tensor(lf[:, 3], gates[:, 1], 0.0, lf[:, 2], ALU.min, ALU.subtract))
                g2.link(dve.tensor_tensor_scan(lf[:, 1], lf[:, 3], lf[:, 3], 0.0, ALU.add, ALU.min))
                ins = dve.tensor_tensor(am[:, 0], gates[:, 0], lf[:, 1], ALU.subtract)
                ins.then_inc(am_ready, 1)
                dve.wait_ge(am_ready, 2 * p + 1)
                g2.link(dve.tensor_tensor_scan(lf[:, 2], am[:, 0], am[:, 0], -3.0e38, ALU.max, ALU.max))
                if not (isinstance(p, int) and p == 0):
                    dve.wait_ge(s_nm, 16 * p)
                dve.tensor_scalar(nm[:], lf[:, 2], -1.0, None, ALU.mult).then_inc(nm_ready, 1)
                dve.scalar_tensor_tensor(am[:, 1], lf[:, 2], -1.0, lf[:, 1], ALU.mult, ALU.subtract
                                         ).then_inc(am_ready, 1)

            def read_a(p):
                dve.wait_ge(back_done, p + 1)
                dve.tensor_copy(aT[:].rearrange("q c n -> q (c n)"), pm[:, 0:4 * NH]).then_inc(aT_ready, 1)

            def products(p, u):
                dve.wait_ge(mask_done, 2 * UNITS * p + 2 * u + 2)
                for blk in range(3):
                    dve.wait_ge(qk_done, 3 * UNITS * p + 3 * u + blk + 1)
                    d = dmat[:, u % 2, blk].rearrange("q h s -> q (h s)")
                    dve.scalar_tensor_tensor(d, pq[:, blk], float(DH) ** -0.5, d, ALU.mult, ALU.mult
                                             ).then_inc(prod_done, 1)

            def post(p):
                link = po_steps.link
                po_steps.start(p)
                sums = tok[:].rearrange("q t h d -> q (t h) d")
                dve.wait_ge(o_read, UNITS * p + UNITS)
                link(dve.scalar_tensor_tensor(hn[:, 0], sums[:, :, DH], -1.0, sums[:, :, DH],
                                              ALU.mult, ALU.max))
                link(dve.tensor_tensor(hn[:, 1], hn[:, 0], floor[:].rearrange("q b c h -> q (b c h)"),
                                       ALU.max))
                link(dve.tensor_scalar(hn[:, 1], hn[:, 1], EPS, None, ALU.add))
                link(dve.tensor_tensor(hn[:, 2], hn[:, 1], hn[:, 1], ALU.mult))
                dve.wait_ge(osq_ready, p + 1)
                link(dve.tensor_reduce(hn[:, 0], osq, AX.X, ALU.add))
                link(dve.tensor_scalar(hn[:, 1], hn[:, 0], 1.0 / DH, None, ALU.mult))
                dve.scalar_tensor_tensor(hn[:, 3], hn[:, 2], EPS, hn[:, 1], ALU.mult, ALU.add
                                         ).then_inc(hvar_ready, 1)
                dve.wait_ge(hvar_ready, p + 1)
                link(dve.tensor_scalar(hn[:, 3], hn[:, 3], VAR_MAX, None, ALU.min))
                link(dve.tensor_scalar(hn[:, 0].bitcast(I32), hn[:, 3].bitcast(I32), 1, None,
                                       ALU.logical_shift_right))
                link(dve.tensor_scalar(hr[:].bitcast(I32), hn[:, 0].bitcast(I32), -1.0, RSQRT_START,
                                       ALU.mult, ALU.add))
                for _ in range(3):
                    link(dve.tensor_tensor(hn[:, 0], hr[:], hr[:], ALU.mult))
                    link(dve.scalar_tensor_tensor(hn[:, 1], hn[:, 0], -0.5, hn[:, 3], ALU.mult, ALU.mult))
                    link(dve.scalar_tensor_tensor(hr[:], hn[:, 1], 1.5, hr[:], ALU.add, ALU.mult))
                dve.wait_ge(s_x, 16 * p + 16)

                def scaled(tt):
                    dve.wait_ge(ols_ready, TT * p + tt + 1)
                    o = tok[:, tt, :, 0:DH]
                    r = hr[:, tt * NH:(tt + 1) * NH].unsqueeze(2).to_broadcast([P, NH, DH])
                    dve.tensor_tensor(o, o, r, ALU.mult).then_inc(oscaled, 1)

                scaled(0)
                for tt in range(TT):
                    if tt + 1 < TT:
                        scaled(tt + 1)
                    dve.wait_ge(oscaled, TT * p + tt + 1)
                    xt = x_sb[:, tt].rearrange("q (h d) -> q h d", d=DH)
                    dve.tensor_tensor(xt, xt, tok[:, tt, :, 0:DH], ALU.add).then_inc(x1_ready, 1)

            def norm2(p):
                for tt in range(TT):
                    dve.wait_ge(x1_ready, TT * p + tt + 1)
                    stats(po_steps, x_sb[:, tt], 1, tt)
                po_steps.wait()
                dve.tensor_scalar(vv[:, 1], mv[:, 1, :, 1], EPS_LN, None, ALU.add).then_inc(var2_ready, 1)
                dve.wait_ge(rstd2_ready, p + 1)
                po_steps.link(dve.tensor_scalar(rk[:], rs[:, 1], PX, None, ALU.mult))
                for tt in range(TT):
                    last = dve.tensor_scalar(yn[:, tt].rearrange("q (w i h) -> q w h i", i=4, h=2),
                                             x_sb[:, tt].rearrange("q (w h i) -> q w h i", i=4, h=2),
                                             mv[:, 1, tt, 0:1], rk[:, tt:tt + 1], ALU.subtract, ALU.mult)
                last.then_inc(yn_ready, 1)

            def low_yT(p):
                for n in range(KT):
                    dve.wait_ge(yh_ready, KT * p + n + 1)
                    dve.tensor_tensor(yT[:, 1, n], pq[:, n % 2], yT[:, 0, n], ALU.subtract
                                      ).then_inc(yl_ready, 1)

            def ffn_up(q, h):
                j, w = h // 2, h % 2
                o = j + w * FT
                acc = ffn[:, 4 + 2 * w + j % 2]
                if w == 1 and j >= 2:
                    dve.wait_ge(h_ready, FT * q + j - 1)
                dve.wait_ge(tsum_ready, 2 * FT * q + h + 1)
                dve.wait_ge(pu_done, 8 * FT * q + 4 * h + 3)
                dve.scalar_tensor_tensor(acc, pf[:, 2], gu_scale[:, 2 * GU + o:2 * GU + o + 1],
                                         ffn[:, 2 * w], ALU.mult, ALU.add).then_inc(acc_ready, 1)
                dve.wait_ge(pu_done, 8 * FT * q + 4 * h + 4)
                dve.wait_ge(acc_ready, 4 * FT * q + 2 * h + 1)
                dve.scalar_tensor_tensor(acc, pf[:, 3], gu_scale[:, 3 * GU + o:3 * GU + o + 1],
                                         acc, ALU.mult, ALU.add).then_inc(acc_ready, 1)

            def gate(q, j):
                dve.wait_ge(th_ready, FT * q + j + 1)
                dve.scalar_tensor_tensor(th[:, j % 2], th[:, j % 2], 1.0, ffn[:, 4 + j % 2],
                                         ALU.add, ALU.mult).then_inc(gg_ready, 1)

            def down(q, half):
                c = slice(2 * half, 2 * half + 2)
                dve.wait_ge(ss_ready, TT * q + 2 * half + 2)
                dve.tensor_scalar(ms[:, c], ssq[:, c], 1.0 / E, EPS, ALU.mult, ALU.add).then_inc(ms_ready, 1)
                dve.wait_ge(yr_ready, 2 * q + half + 1)
                dve.wait_ge(s_res, 16 * q + 16)
                for tt in range(2 * half, 2 * half + 2):
                    dve.scalar_tensor_tensor(x_res[:, tt], pf[:, tt], yr[:, tt:tt + 1], x_res[:, tt],
                                             ALU.mult, ALU.add).then_inc(o_ready, 1)

            own = [0]

            def step(ins):
                ins.then_inc(dve_w, 1)
                own[0] += 1
                dve.wait_ge(dve_w, own[0])

            def decode(words, dst, a, bb):
                for i in range(4):
                    step(dve.tensor_scalar(a, words, 12 - 4 * i, SIGN_MASK, ALU.logical_shift_left,
                                           ALU.bitwise_and))
                    if i < 3:
                        step(dve.tensor_scalar(bb, words, 9 - 4 * i, MAGN_MASK, ALU.logical_shift_left,
                                               ALU.bitwise_and))
                    else:
                        step(dve.tensor_scalar(bb, words, 3, MAGN_MASK, ALU.logical_shift_right,
                                               ALU.bitwise_and))
                    step(dve.tensor_tensor(dst(i), a, bb, ALU.bitwise_or))
                dve.sem_inc(fp4_ready, 1)

            def gate_weights():
                dve.wait_ge(s_const, 16 * 7)
                dve.tensor_tensor(w_gate[:, KT:2 * KT], w_gate[:, KT:2 * KT], w_gate[:, 2 * KT:3 * KT],
                                  ALU.add).then_inc(wg_ready, 1)

            def prepare(j):
                if j < 2:
                    dve.wait_ge(s_words, 32)
                    o = slice(j * FT, (j + 1) * FT)
                    a, bb = (bits[:, k * FT * NW:(k + 1) * FT * NW].rearrange("q (o w) -> q o w", o=FT)
                             for k in range(2))
                    decode(gu_words[:, o], lambda i: gu_bits[:, o, :, i], a, bb)
                if j == 2:
                    dve.wait_ge(xT_done, KT)
                    a, bb = (bits[:, k * KT * DW:(k + 1) * KT * DW].rearrange("q (o w) -> q o w", o=KT)
                             for k in range(2))
                    decode(dn_words, lambda i: dn_bits[:, :, :, i], a, bb)
                if j == 3:
                    dve.wait_ge(gut_done, FT)
                    dve.wait_ge(sc_ready, 3)
                    for o in range(KT):
                        for i in range(4):
                            s = dn_scale[:].rearrange("q (g o) -> q g o", o=KT)[:, :, o]
                            dve.tensor_tensor(
                                dn_f32[:, o].rearrange("q (g w h i) -> q i g w h", g=FT, h=2, i=4)[:, i],
                                dn_fp4[:, o, i], s.unsqueeze(2).unsqueeze(3).to_broadcast([P, FT, 16, 2]),
                                ALU.mult).then_inc(dn32_ready, 1)

            def iteration(p, q, n):
                for h in range(GU):
                    if p is not None and h in PRODUCTS:
                        products(p, PRODUCTS[h])
                    if q is not None:
                        if h % 2 == 0 and h > 0:
                            gate(q, h // 2 - 1)
                        ffn_up(q, h)
                    elif h % 2 == 0 and h > 0:
                        prepare(h // 2)
                    if p is not None and h in SPREAD:
                        spread_q(p, SPREAD[h])
                if q is not None:
                    gate(q, FT - 1)
                if p is not None:
                    post(p)
                    norm2(p)
                    low_yT(p)
                if n is not None:
                    norm1(n)
                if q is not None:
                    down(q, 0)
                if n is not None:
                    spread_q(n, 0)
                    spread_q(n, 1)
                    gate_bias(n)
                    abs_f(n)
                    scans(n)
                    read_a(n)
                if q is not None:
                    down(q, 1)

            norm1(0)
            gate_weights()
            prepare(0)
            spread_q(0, 0)
            spread_q(0, 1)
            gate_bias(0)
            abs_f(0)
            scans(0)
            read_a(0)
            iteration(0, None, 1)
            dve.sem_inc(o_ready, TT)
            with dve.Fori(1, PAIRS - 1) as p:
                iteration(p, p - 1, p + 1)
            iteration(PAIRS - 1, PAIRS - 2, None)
            iteration(None, PAIRS - 1, None)


_INS = ["x", "ctx_2048", "L0_xattn_Wi", "L0_xattn_bi", "L0_xattn_Wf", "L0_xattn_bf", "L0_xattn_ln_scale",
        "L0_ffn_gate_up_packed", "L0_ffn_gate_up_scales", "L0_ffn_down_packed", "L0_ffn_down_scales"]


def kernel(**inputs):
    import numpy as _np
    import concourse.bacc as _bacc
    from concourse import mybir as _mybir
    from concourse.bass_utils import run_bass_kernel_spmd as _run

    nc = _bacc.Bacc("TRN2", target_bir_lowering=False, num_devices=1)
    arrays, args = {}, []
    for name in _INS:
        a = _np.ascontiguousarray(inputs[name])
        arrays[f"in_{name}"] = a
        args.append(nc.dram_tensor(f"in_{name}", a.shape, _mybir.dt.from_np(a.dtype), kind="ExternalInput").ap())
    args.append(nc.dram_tensor("out_0", (B, S, E), F32, kind="ExternalOutput").ap())
    xattn_ffn(nc, *args)
    r = _run(nc, [arrays], core_ids=[0])
    return r.results[0]["out_0"]
```

```python
from contextlib import ExitStack

import concourse.bass as bass
from concourse import mybir

F32 = mybir.dt.float32
F16 = mybir.dt.float16
I32 = mybir.dt.int32
ALU = mybir.AluOpType
ACT = mybir.ActivationFunctionType
AX = mybir.AxisListType

P = 128
B, S, E, NH = 8, 256, 512, 16
DH = E // NH
PAIRS = B // 2
TT = 2 * S // P
KT = E // P
HG = P // DH
I = 1408
FT = I // P
GU = 2 * FT
NW = E // 8
DW = I // 8
BLKS = 2
UNITS = 2 * KT
PX = 1024.0
EPS_LN = 1e-5
EPS = 1e-6
FP4_SCALE = 16384.0
SIGN_MASK = 0x80008000 - (1 << 32)
MAGN_MASK = 0x0E000E00
VAR_MAX = 1e38
RSQRT_START = float(0x5F3759DF)
GROWS = DH + NH

SCORES_AT = tuple(2 * u + 1 for u in range(UNITS))
SCORES = {h: u for u, h in enumerate(SCORES_AT)}
EXPS = {h - 2: u for u, h in enumerate(SCORES_AT) if u}
MASKS = {0: 0, **EXPS}
VALUES = {h + 1: u for u, h in enumerate(SCORES_AT)}
READ_O = {h + 2: u for u, h in enumerate(SCORES_AT)}
ADD = {h + 2: u for u, h in enumerate(SCORES_AT)}
SPREAD = {SCORES_AT[1] + 3: 2, SCORES_AT[3] + 3: 3}
SQUARES = {SCORES_AT[-2] + 3: 0, SCORES_AT[-1] + 3: 1}
SPARE = 19
TURNS = (*range(KT, 2 * KT), *range(KT))
PARTS = ((0, 1), (2,), (3,))
BEFORE_TURNS, BEFORE_BACK = 5, 5
GU_PREP = {0: range(5), 1: range(5, 7), 2: range(7, 9), 3: range(9, FT)}
DN_PREP = {6: range(4), 7: range(4, 8), 8: range(8, FT)}
DN_WORDS_AT = 2


class Chain:

    def __init__(self, eng, sem):
        self.eng, self.sem, self.per, self.n, self.base = eng, sem, None, 0, 0

    def start(self, p):
        if self.per is None and self.n:
            self.per = self.n
        self.base = 0 if self.per is None else p * self.per
        self.n = 0

    def inc(self, ins):
        ins.then_inc(self.sem, 1)
        self.n += 1

    def wait(self):
        self.eng.wait_ge(self.sem, self.base + self.n)

    def link(self, ins):
        self.inc(ins)
        self.wait()


def xattn_ffn(nc, x, ctx, Wi, bi, Wf, bf, ln_scale, gu_packed, gu_scales, dn_packed, dn_scales, out):
    x_pairs = x.rearrange("(p b) (c q) d -> p q (b c) d", b=2, q=P)
    ctx_pairs = ctx.rearrange("(p b) (c q) d -> p q (b c) d", b=2, q=P)
    out_pairs = out.rearrange("(p b) (c q) d -> p q (b c) d", b=2, q=P)
    negm_dram = nc.dram_tensor("negm_dram", (2 * NH, S), F32, kind="Internal").ap()

    es = ExitStack()
    with es:
        def sb(name, shape, dt=F32):
            return es.enter_context(nc.sbuf_tensor(name, shape, dt))

        def sem(name):
            return es.enter_context(nc.semaphore(name))

        ident = sb("ident", [P, P])
        ident16 = sb("ident16", [P, P], F16)
        neghalf = sb("neghalf", [P, TT])
        bias_col = sb("bias_col", [GROWS, 1])
        ln_row = sb("ln_row", [P, E])
        w_gate = sb("w_gate", [P, 3 * KT, GROWS])
        gu_val = sb("gu_val", [P, GU, KT, P], F16)
        w_down = sb("w_down", [P, FT, E])
        gu_scale = sb("gu_scale", [P, KT * GU])
        dn_scale = sb("dn_scale", [P, FT * KT])
        sc_raw = sb("sc_raw", [KT * GU, P], F16)
        dsc_raw = sb("dsc_raw", [FT * KT, P], F16)
        x_sb = sb("x_sb", [P, TT, E])
        x_res = sb("x_res", [P, TT, E])
        ctx_sb = sb("ctx_sb", [P, TT, E])
        tok = sb("tok", [P, TT, NH, DH + 1])
        xT = sb("xT", [P, 2 * KT, TT * P])
        v_sb = sb("v_sb", [P, TT, NH, DH + 1])
        q_diag = sb("q_diag", [P, 2, HG, TT * P])
        negm = sb("negm", [P, 4, HG, S])
        dmat = sb("dmat", [P, 2, BLKS, HG, P])
        vw = sb("vw", [P, 2, HG, DH + 1])
        state = sb("state", [P, 2, HG, DH + 1])
        own_rows = sb("own_rows", [P, HG, DH + 1])
        later = sb("later", [P, 2, HG, DH + 1])
        decay = sb("decay", [P, 2, NH])
        yT = sb("yT", [P, 2, KT, TT * P], F16)
        ffn = sb("ffn", [P, 8, TT * P])
        th = sb("th", [P, 2, TT * P])
        hT = sb("hT", [P, FT, TT * P])
        gates = negm[0:NH, 0].rearrange("q h s -> q (h s)").rearrange("q (g s) -> q g s", g=2)
        am = negm[0:NH, 1].rearrange("q h s -> q (h s)").rearrange("q (g s) -> q g s", g=2)
        lf = negm[0:NH, 2:4].rearrange("q u h s -> q (u h s)").rearrange("q (g s) -> q g s", g=4)
        nm = sb("nm", [NH, TT * P])
        aT = sb("aT", [P, 2, 2 * NH])
        floor = sb("floor", [P, 2, 2, NH])
        bst = sb("bst", [P, 2, TT, 6])
        mv = sb("mv", [P, 2, TT, 2])
        vv = sb("vv", [P, 2, TT])
        rs = sb("rs", [P, 2, TT])
        rk = sb("rk", [P, TT])
        vmean = sb("vmean", [P, 2, TT * NH])
        hn = sb("hn", [P, 4, TT * NH])
        hr = sb("hr", [P, TT * NH])
        ssq = sb("ssq", [P, TT])
        ms = sb("ms", [P, TT])
        yr = sb("yr", [P, TT])
        gu_words = x_res[:].rearrange("p a b -> p (a b)").bitcast(I32)[:, 0:GU * NW].rearrange(
            "p (o w) -> p o w", o=GU)
        dn_words = th[:].rearrange("p a b -> p (a b)").bitcast(I32)[:, 0:KT * DW].rearrange(
            "p (o w) -> p o w", o=KT)
        bits = yT[:].rearrange("p a b c -> p (a b c)").bitcast(I32)
        gu_bits = hT[:].rearrange("p a b -> p (a b)").bitcast(I32).rearrange(
            "p (o w i) -> p o w i", o=GU, i=4)
        gu_fp4 = hT[:].rearrange("p a b -> p (a b)").bitcast(F16).rearrange(
            "p (o k) -> p o k", o=GU)
        dn_bits = ffn[:].rearrange("p a b -> p (a b)").bitcast(I32)[:, 0:KT * 4 * DW].rearrange(
            "p (o w i) -> p o w i", o=KT, i=4)
        dn_fp4 = ffn[:].rearrange("p a b -> p (a b)").bitcast(F16)[:, 0:KT * I].rearrange(
            "p (o g w i h) -> p o i g w h", o=KT, g=FT, i=4, h=2)
        dn_f32 = hT[:].rearrange("p a b -> p (a b)").rearrange("p (o k) -> p o k", o=KT)
        xg = ffn[:, 0:TT]
        yn = tok[:].rearrange("p a b c -> p a (b c)")[:, :, 0:E]
        osq = dmat[:].rearrange("p a b c d -> p (a b c d)")[:, 0:TT * E].rearrange(
            "p (g d) -> p g d", d=DH)

        pf = es.enter_context(nc.psum_tensor("pf", [P, 4, 512], F32))
        pq = es.enter_context(nc.psum_tensor("pq", [P, 3, 512], F32))
        po = es.enter_context(nc.psum_tensor("po", [P, 512], F32))
        pm = pq[:, 2]

        def spare(q, h):
            if isinstance(q, int) and q == PAIRS - 1:
                return h % 2 == 1
            return h == 0 or h % 2 == 1 and h >= SPARE

        def bank(q, h, g):
            if spare(q, h):
                return pq[:, g] if g < 3 else po[:]
            return pf[:, g]

        def bank_y(p, n):
            if isinstance(p, int) and p == 0:
                return pq[:, n % 2]
            return pq[:, 2] if n % 2 == 0 else po[:]

        s_const = sem("s_const")
        s_words = sem("s_words")
        s_x = sem("s_x")
        s_xg = sem("s_xg")
        s_ctx = sem("s_ctx")
        s_res = sem("s_res")
        s_nm = sem("s_nm")
        s_negm = [sem(f"s_negm{i}") for i in range(4)]
        s_out = sem("s_out")
        const_ready = sem("const_ready")
        wg_ready = sem("wg_ready")
        sc_done = sem("sc_done")
        sc_ready = sem("sc_ready")
        fp4_ready = sem("fp4_ready")
        gut_done = sem("gut_done")
        gut_read = sem("gut_read")
        dn32_ready = sem("dn32_ready")
        dnt_done = sem("dnt_done")
        dnt_read = sem("dnt_read")
        waits_taken = sem("waits_taken")
        dve_w = sem("dve_w")
        dve_g1 = sem("dve_g1")
        dve_g2 = sem("dve_g2")
        dve_p = sem("dve_p")
        act_g = sem("act_g")
        var1_ready = sem("var1_ready")
        rstd1_ready = sem("rstd1_ready")
        xn_ready = sem("xn_ready")
        vmean_ready = sem("vmean_ready")
        v_ready = sem("v_ready")
        xT_done = sem("xT_done")
        xT_read = sem("xT_read")
        g_done = sem("g_done")
        absf_ready = sem("absf_ready")
        softp_ready = sem("softp_ready")
        nm_ready = sem("nm_ready")
        am_ready = sem("am_ready")
        back_done = sem("back_done")
        aT_ready = sem("aT_ready")
        floor_ready = sem("floor_ready")
        qdiag_ready = sem("qdiag_ready")
        qk_done = sem("qk_done")
        vw_ready = sem("vw_ready")
        st_done = sem("st_done")
        state_ready = sem("state_ready")
        later_ready = sem("later_ready")
        o_whole = sem("o_whole")
        exp_done = sem("exp_done")
        mask_done = sem("mask_done")
        prod_done = sem("prod_done")
        pv_done = sem("pv_done")
        o_read = sem("o_read")
        osq_ready = sem("osq_ready")
        oscaled = sem("oscaled")
        hvar_ready = sem("hvar_ready")
        ols_ready = sem("ols_ready")
        x1_ready = sem("x1_ready")
        var2_ready = sem("var2_ready")
        rstd2_ready = sem("rstd2_ready")
        yn_ready = sem("yn_ready")
        yT_done = sem("yT_done")
        yh_ready = sem("yh_ready")
        yl_ready = sem("yl_ready")
        pu_done = sem("pu_done")
        t_ready = sem("t_ready")
        tsum_ready = sem("tsum_ready")
        acc_ready = sem("acc_ready")
        th_ready = sem("th_ready")
        gg_ready = sem("gg_ready")
        h_ready = sem("h_ready")
        dn_done = sem("dn_done")
        ss_ready = sem("ss_ready")
        ms_ready = sem("ms_ready")
        yr_ready = sem("yr_ready")
        o_ready = sem("o_ready")

        def take_wait(eng):
            eng.sem_inc(waits_taken, 1)

        block = es.enter_context(nc.Block())

        @block.sync
        def _(sp):
            def load_ctx(p):
                if not (isinstance(p, int) and p == 0):
                    sp.wait_ge(st_done, UNITS * p)
                    take_wait(sp)
                    sp.wait_ge(xT_done, 2 * KT * p)
                    take_wait(sp)
                    sp.wait_ge(v_ready, TT * p)
                sp.dma_start(ctx_sb[:], ctx_pairs[p]).then_inc(s_ctx, 16)

            def load_xg(p, q):
                if q is not None:
                    sp.wait_ge(acc_ready, 4 * FT * q + 4 * FT)
                elif p > 0:
                    sp.wait_ge(dn32_ready, 4 * KT)
                sp.dma_start(xg, x_pairs[p]).then_inc(s_xg, 16)

            def load_x(p):
                sp.dma_start(x_sb[:], x_pairs[p]).then_inc(s_x, 16)

            def keep_residual(q):
                sp.wait_ge(yn_ready, q + 1)
                take_wait(sp)
                sp.wait_ge(x1_ready, 4 * q + 4)
                take_wait(sp)
                sp.dma_start(x_res[:], x_sb[:]).then_inc(s_res, 16)
                sp.wait_ge(s_res, 16 * q + 16)
                take_wait(sp)

            def spread_negm(p):
                sp.wait_ge(nm_ready, p + 1)
                take_wait(sp)
                if not (isinstance(p, int) and p == 0):
                    sp.wait_ge(exp_done, UNITS * p)
                sp.dma_start(negm_dram.rearrange("(b h) s -> h b s", b=2),
                             nm[:].rearrange("h (b s) -> h b s", b=2)).then_inc(s_nm, 16)
                sp.wait_ge(s_nm, 16 * p + 16)
                take_wait(sp)
                load_units(range(1))
                sp.wait_ge(back_done, p + 1)
                take_wait(sp)
                load_units(range(1, 4))

            def late_negm(p):
                for u in range(4, UNITS):
                    sp.wait_ge(exp_done, UNITS * p + u - 3)
                    load_units((u,))

            def load_units(units):
                for u in units:
                    hg, b = u // 2, u % 2
                    r = b * NH + hg * HG
                    sp.dma_start(negm[:, u % 4].rearrange("q h s -> q (h s)"),
                                 negm_dram[r:r + HG, :].rearrange("h s -> (h s)").partition_broadcast(P)
                                 ).then_inc(s_negm[u % 4], 16)

            def store(q, tiles):
                for tt in tiles:
                    sp.wait_ge(o_ready, TT * (q + 1) + tt + 1)
                    sp.dma_start(out_pairs[q][:, tt], x_res[:, tt]).then_inc(s_out, 16)
                if tt == TT - 1:
                    sp.wait_ge(s_out, 16 * TT * q + 16 * TT)
                    take_wait(sp)

            def iteration(p, q, n):
                if q is not None:
                    keep_residual(q)
                if p is not None:
                    load_x(p)
                    late_negm(p)
                    if q is None:
                        load_xg(n, q)
                    if n is not None:
                        load_ctx(n)
                if n is not None and q is not None:
                    load_xg(n, q)
                if q is not None:
                    store(q, range(2))
                if n is not None:
                    spread_negm(n)
                if q is not None:
                    store(q, range(2, TT))

            load_xg(0, None)
            load_ctx(0)
            for i, w in enumerate((Wi, Wf)):
                sp.dma_start(w_gate[:, :, i * DH:i * DH + NH], w.rearrange("(k q) h -> q k h", q=P)
                             ).then_inc(s_const, 16)
            for i, v in enumerate((bi, bf)):
                sp.dma_start(bias_col[i * DH:i * DH + NH], v.rearrange("(h o) -> h o", o=1)
                             ).then_inc(s_const, 16)
            sp.dma_start(ln_row[:], ln_scale.partition_broadcast(P)).then_inc(s_const, 16)
            sp.dma_start(sc_raw[:], gu_scales.rearrange("g (o q) -> (g o) q", q=P)).then_inc(s_const, 16)
            sp.dma_start(dsc_raw[:], dn_scales.rearrange("g (o q) -> (g o) q", q=P)).then_inc(s_const, 16)
            sp.dma_start(gu_words, gu_packed.rearrange("(o q) w -> q o w", q=P)).then_inc(s_words, 16)
            sp.dma_start(dn_words, dn_packed.rearrange("(o q) w -> q o w", q=P)).then_inc(s_words, 16)
            spread_negm(0)
            iteration(0, None, 1)
            sp.wait_ge(fp4_ready, 3)
            with sp.Fori(1, PAIRS - 1) as p:
                iteration(p, p - 1, p + 1)
            iteration(PAIRS - 1, PAIRS - 2, None)
            iteration(None, PAIRS - 1, None)

        @block.gpsimd
        def _(pool):
            def setup():
                pool.memset(ident[:], 0.0).then_inc(const_ready, 1)
                pool.wait_ge(const_ready, 1)
                pool.affine_select(out=ident[:], in_=ident[:], compare_op=ALU.not_equal, fill=1.0, base=0,
                                   pattern=[[-1, P]], channel_multiplier=1).then_inc(const_ready, 1)
                pool.wait_ge(const_ready, 2)
                pool.tensor_copy(ident16[:], ident[:]).then_inc(const_ready, 1)
                pool.memset(neghalf[:], -0.5).then_inc(const_ready, 1)
                pool.memset(v_sb[:, :, :, DH:DH + 1], 1.0).then_inc(const_ready, 1)
                pool.memset(q_diag[:], 0.0).then_inc(const_ready, 1)
                pool.memset(w_gate[:, :, NH:DH], 0.0).then_inc(const_ready, 1)
                pool.memset(own_rows[:], float(DH) ** -0.5).then_inc(const_ready, 1)
                pool.wait_ge(const_ready, 8)
                pool.affine_select(out=own_rows[:], in_=own_rows[:], compare_op=ALU.is_ge, fill=0.0, base=0,
                                   pattern=[[-DH, HG], [0, DH + 1]], channel_multiplier=1
                                   ).then_inc(const_ready, 1)
                pool.wait_ge(const_ready, 9)
                pool.affine_select(out=own_rows[:], in_=own_rows[:], compare_op=ALU.is_ge, fill=0.0,
                                   base=DH - 1, pattern=[[DH, HG], [0, DH + 1]], channel_multiplier=-1
                                   ).then_inc(const_ready, 1)
                pool.wait_ge(const_ready, 10)

            def rstd1(p):
                pool.wait_ge(var1_ready, p + 1)
                pool.tensor_tensor(rs[:, 0], vv[:, 0], neghalf[:, 0:TT], ALU.pow).then_inc(rstd1_ready, 1)

            def centre_v(p):
                pool.wait_ge(vmean_ready, p + 1)
                pool.wait_ge(s_ctx, 16 * p + 16)
                if not (isinstance(p, int) and p == 0):
                    pool.wait_ge(pv_done, UNITS * p)
                for tt in range(TT):
                    m = vmean[:, 1, tt * NH:(tt + 1) * NH].unsqueeze(2).to_broadcast([P, NH, DH])
                    pool.tensor_tensor(v_sb[:, tt, :, 0:DH],
                                       ctx_sb[:, tt].rearrange("q (h d) -> q h d", d=DH), m, ALU.add
                                       ).then_inc(v_ready, 1)

            def mask(p, u):
                pool.wait_ge(exp_done, UNITS * p + u + 1)
                take_wait(pool)
                for blk in range(BLKS):
                    d = dmat[:, u % 2, blk]
                    pool.affine_select(out=d, in_=d, compare_op=ALU.is_ge, fill=0.0, base=0,
                                       pattern=[[0, HG], [1, P]], channel_multiplier=-1
                                       ).then_inc(mask_done, 1)
                hg, b = u // 2, u % 2
                if u == 0:
                    pool.wait_ge(v_ready, TT * p + TT)
                pool.wait_ge(mask_done, 2 * UNITS * p + 2 * u + 1)
                pool.tensor_tensor(vw[:, u % 2], v_sb[:, 2 * b, hg * HG:(hg + 1) * HG, :],
                                   dmat[:, u % 2, 0, :, P - 1:P].to_broadcast([P, HG, DH + 1]), ALU.mult
                                   ).then_inc(vw_ready, 1)

            def post(p):
                if isinstance(p, int) and p == 0:
                    pool.wait_ge(s_const, 16 * 7)
                for tt in range(TT):
                    pool.wait_ge(osq_ready, 2 * p + 1 + tt // 2)
                    o = tok[:, tt, :, 0:DH]
                    pool.tensor_tensor(o, o, ln_row[:].rearrange("q (h d) -> q h d", d=DH), ALU.mult
                                       ).then_inc(ols_ready, 1)
                pool.wait_ge(s_x, 16 * p + 16)
                for tt in range(TT):
                    pool.wait_ge(oscaled, TT * p + tt + 1)
                    xt = x_sb[:, tt].rearrange("q (h d) -> q h d", d=DH)
                    pool.tensor_tensor(xt, xt, tok[:, tt, :, 0:DH], ALU.add).then_inc(x1_ready, 1)

            def norm2(p):
                pool.wait_ge(var2_ready, p + 1)
                pool.tensor_tensor(rs[:, 1], vv[:, 1], neghalf[:, 0:TT], ALU.pow).then_inc(rstd2_ready, 1)

            def sum_t(q, h):
                pool.wait_ge(t_ready, 4 * FT * q + 2 * h + 2)
                t = ffn[:, 2 * (h % 2)]
                pool.tensor_tensor(t, t, ffn[:, 2 * (h % 2) + 1], ALU.add).then_inc(tsum_ready, 1)

            def gated(q, j):
                pool.wait_ge(acc_ready, 4 * FT * q + 4 * j + 4)
                pool.wait_ge(gg_ready, FT * q + j + 1)
                pool.tensor_tensor(hT[:, j], ffn[:, 6 + j % 2], th[:, j % 2], ALU.mult
                                   ).then_inc(h_ready, 1)

            def down(q, part):
                pool.wait_ge(ms_ready, 3 * q + part + 1)
                c = slice(PARTS[part][0], PARTS[part][-1] + 1)
                pool.tensor_tensor(yr[:, c], ms[:, c], neghalf[:, c], ALU.pow).then_inc(yr_ready, 1)

            def iteration(p, q, n):
                for h in range(GU):
                    if q is not None:
                        sum_t(q, h)
                        if h % 2 == 1 and h > 1:
                            gated(q, h // 2 - 1)
                    if p is not None and h in MASKS:
                        mask(p, MASKS[h])
                    if q is None and h == 14:
                        rstd1(n)
                if q is None:
                    post(p)
                    norm2(p)
                    centre_v(n)
                    return
                if q is not None:
                    gated(q, FT - 1)
                if p is not None:
                    post(p)
                if n is not None:
                    rstd1(n)
                if p is not None:
                    norm2(p)
                if q is not None:
                    down(q, 0)
                if n is not None:
                    centre_v(n)
                if q is not None:
                    down(q, 1)
                    down(q, 2)

            setup()
            rstd1(0)
            centre_v(0)
            iteration(0, None, 1)
            with pool.Fori(1, PAIRS - 1) as p:
                iteration(p, p - 1, p + 1)
            iteration(PAIRS - 1, PAIRS - 2, None)
            iteration(None, PAIRS - 1, None)

        @block.scalar
        def _(act):
            chain = Chain(act, act_g)

            def read_xT(p, half):
                for m in range(half * KT, half * KT + KT):
                    n = TURNS[m]
                    act.wait_ge(xT_done, 2 * KT * p + m + 1)
                    if m == 0 and not (isinstance(p, int) and p == 0):
                        act.wait_ge(qdiag_ready, NH * p)
                        act.wait_ge(qk_done, BLKS * UNITS * p)
                        act.wait_ge(pv_done, UNITS * p)
                    act.activation(xT[:, n], pq[:, m % 2], ACT.Copy).then_inc(xT_read, 1)

            def softplus(p):
                chain.start(p)
                act.wait_ge(absf_ready, p + 1)
                chain.link(act.activation(lf[:, 1], lf[:, 0], ACT.Exp, scale=-1.0))
                act.activation(lf[:, 2], lf[:, 1], ACT.Ln, bias=1.0).then_inc(softp_ready, 1)

            def floors(p):
                act.wait_ge(aT_ready, p + 1)
                if not (isinstance(p, int) and p == 0):
                    act.wait_ge(hvar_ready, p)
                act.activation(floor[:].rearrange("q b c h -> q c b h"),
                               pm[:, 4 * NH:8 * NH].rearrange("q (c b h) -> q c b h", c=2, b=2),
                               ACT.Exp).then_inc(floor_ready, 1)
                act.activation(decay[:].rearrange("q b h -> q (b h)"), pm[:, 8 * NH:10 * NH], ACT.Exp
                               ).then_inc(floor_ready, 1)

            def exps(p, u):
                hg, b = u // 2, u % 2
                act.wait_ge(s_negm[u % 4], 32 * p + 16 * (u // 4) + 16)
                act.wait_ge(aT_ready, p + 1)
                if u >= 2:
                    act.wait_ge(pv_done, UNITS * p + u - 1)
                elif not (isinstance(p, int) and p == 0):
                    act.wait_ge(hvar_ready, p)
                for h in range(HG):
                    bh = b * NH + hg * HG + h
                    for c in range(BLKS):
                        last = act.activation(dmat[:, u % 2, c, h], negm[:, u % 4, h, c * P:(c + 1) * P],
                                              ACT.Exp, bias=aT[:, c, bh:bh + 1])
                last.then_inc(exp_done, 1)

            def read_o(p, u):
                hg, b = u // 2, u % 2
                act.wait_ge(pv_done, UNITS * p + u + 1)
                act.activation(tok[:, 2 * b:2 * b + 2, hg * HG:(hg + 1) * HG, :].rearrange(
                                   "q c h d -> q c (h d)"),
                               po[:, 0:2 * HG * (DH + 1)].rearrange("q (c n) -> q c n", c=2),
                               ACT.Copy).then_inc(o_read, 1)

            def squares(p, b):
                act.wait_ge(o_whole, UNITS * p + UNITS - 1 + b)
                act.wait_ge(pv_done, UNITS * p + UNITS - 1 + b)
                g = slice(b * 2 * NH, (b + 1) * 2 * NH)
                act.activation(osq[:, g], tok[:].rearrange("q t h d -> q (t h) d")[:, g, 0:DH], ACT.Square
                               ).then_inc(osq_ready, 1)

            def read_yT(p):
                for n in range(KT):
                    act.wait_ge(yT_done, KT * p + n + 1)
                    if n == 0 and not (isinstance(p, int) and p == 0):
                        act.wait_ge(pu_done, 8 * FT * p)
                    act.activation(yT[:, 0, n], bank_y(p, n), ACT.Copy).then_inc(yh_ready, 1)

            def scale_t(q, h):
                o = h // 2 + h % 2 * FT
                if h >= 2:
                    act.wait_ge(acc_ready, 4 * FT * q + 2 * h - 3)
                for g in range(2):
                    act.wait_ge(pu_done, 8 * FT * q + 4 * h + g + 1)
                    act.activation(ffn[:, 2 * (h % 2) + g], bank(q, h, g), ACT.Copy,
                                   scale=gu_scale[:, g * GU + o:g * GU + o + 1]).then_inc(t_ready, 1)

            def tanh(q, j):
                act.wait_ge(acc_ready, 4 * FT * q + 4 * j + 2)
                if j >= 2:
                    act.wait_ge(h_ready, FT * q + j - 1)
                act.activation(th[:, j % 2], ffn[:, 4 + j % 2], ACT.Tanh, scale=0.5).then_inc(th_ready, 1)

            def down(q, tt):
                act.wait_ge(dn_done, TT * q + tt + 1)
                if tt == 0:
                    act.wait_ge(h_ready, FT * q + FT)
                if tt > 0:
                    act.wait_ge(ss_ready, TT * q + tt)
                act.activation(th[:, 0], pf[:, tt], ACT.Square, accum_out=ssq[:, tt:tt + 1]
                               ).then_inc(ss_ready, 1)

            def read_scales():
                act.wait_ge(sc_done, 1)
                act.activation(gu_scale[:].rearrange("q (g w o) -> q g w o", g=KT, w=2)[:, :, 0],
                               pf[:, 0].bitcast(F16)[:, 0:KT * GU].rearrange(
                                   "q (g w o) -> q g w o", g=KT, w=2)[:, :, 0],
                               ACT.Copy, scale=1.0 / PX).then_inc(sc_ready, 1)
                act.activation(gu_scale[:].rearrange("q (g w o) -> q g w o", g=KT, w=2)[:, :, 1],
                               pf[:, 0].bitcast(F16)[:, 0:KT * GU].rearrange(
                                   "q (g w o) -> q g w o", g=KT, w=2)[:, :, 1],
                               ACT.Copy, scale=0.5 / PX).then_inc(sc_ready, 1)
                act.activation(dn_scale[:], pf[:, 1].bitcast(F16)[:, 0:FT * KT], ACT.Copy,
                               scale=FP4_SCALE).then_inc(sc_ready, 1)

            def prepare(j):
                for n in GU_PREP.get(j, ()):
                    act.wait_ge(gut_done, n + 1)
                    act.activation(gu_val[:, 2 * n:2 * n + 2].rearrange("q o g k -> q (o g k)"),
                                   pf[:, n % 4].bitcast(F16), ACT.Copy, scale=FP4_SCALE).then_inc(gut_read, 1)
                for n in DN_PREP.get(j, ()):
                    act.wait_ge(dnt_done, n + 1)
                    act.activation(w_down[:, n], pf[:, n % 4], ACT.Copy).then_inc(dnt_read, 1)

            def iteration(p, q, n):
                for h in range(GU):
                    if q is not None:
                        scale_t(q, h)
                    elif h % 2 == 0 and h > 0:
                        prepare(h // 2)
                    if p is not None and h in READ_O:
                        read_o(p, READ_O[h])
                    if q is not None:
                        if h % 2 == 0 and h > 0:
                            tanh(q, h // 2 - 1)
                    if p is not None:
                        if h in EXPS:
                            exps(p, EXPS[h])
                        if h in SQUARES:
                            squares(p, SQUARES[h])
                if q is not None:
                    tanh(q, FT - 1)
                if q is not None:
                    down(q, 0)
                    down(q, 1)
                if n is not None:
                    read_xT(n, 0)
                if p is not None and q is not None:
                    read_yT(p)
                if n is not None:
                    read_xT(n, 1)
                    softplus(n)
                if q is not None:
                    down(q, 2)
                if q is None:
                    read_yT(p)
                if n is not None:
                    floors(n)
                    exps(n, 0)
                if q is not None:
                    down(q, 3)

            read_xT(0, 0)
            read_xT(0, 1)
            read_scales()
            softplus(0)
            prepare(0)
            floors(0)
            exps(0, 0)
            iteration(0, None, 1)
            with act.Fori(1, PAIRS - 1) as p:
                iteration(p, p - 1, p + 1)
            iteration(PAIRS - 1, PAIRS - 2, None)
            iteration(None, PAIRS - 1, None)

        @block.tensor
        def _(pe):
            def turn_x(p, half):
                first = isinstance(p, int) and p <= 1
                for m in range(half * KT, half * KT + KT):
                    n = TURNS[m]
                    if m == 0:
                        pe.wait_ge(s_ctx, 16 * p + 16)
                        if not (isinstance(p, int) and p == 0):
                            pe.wait_ge(prod_done, BLKS * UNITS * p)
                            pe.wait_ge(later_ready, UNITS * p)
                        if not first:
                            pe.wait_ge(t_ready, 4 * FT * (p - 1))
                    if m == KT:
                        pe.wait_ge(xn_ready, p + 1)
                    if m >= 2:
                        pe.wait_ge(xT_read, 2 * KT * p + m - 1)
                    for tt in range(TT):
                        c = slice((n % KT) * P, (n % KT + 1) * P)
                        src = xg[:, tt, c] if n < KT else ctx_sb[:, tt, c]
                        last = pe.transpose(pq[:, m % 2, tt * P:(tt + 1) * P], src, ident[:])
                    last.then_inc(xT_done, 1)

            def gate_sums(p):
                pe.wait_ge(xT_read, 2 * KT * (p + 1))
                if isinstance(p, int) and p == 0:
                    pe.wait_ge(wg_ready, 1)
                elif not (isinstance(p, int) and p == 1):
                    pe.wait_ge(yh_ready, KT * p)
                    pe.wait_ge(yl_ready, KT * p)
                for k in range(2 * KT):
                    last = pe.matmul(pm[0:GROWS, :], w_gate[:, k], xT[:, k],
                                     start=(k == 0), stop=(k == 2 * KT - 1))
                last.then_inc(g_done, 1)

            def turn_back(p):
                pe.wait_ge(am_ready, 2 * p + 2)
                take_wait(pe)
                for w in range(2):
                    for c in range(2):
                        for b in range(2):
                            k = (2 * (2 * w + c) + b) * NH
                            last = pe.transpose(pm[:, k:k + NH], am[:, w, b * S + c * P:b * S + (c + 1) * P],
                                                ident[0:NH, 0:NH])
                for b in range(2):
                    last = pe.transpose(pm[:, (8 + b) * NH:(9 + b) * NH], lf[:, 0, b * S + P:(b + 1) * S],
                                        ident[0:NH, 0:NH])
                last.then_inc(back_done, 1)

            def scores(p, q, u):
                hg, b = u // 2, u % 2
                pe.wait_ge(qdiag_ready, NH * p + HG * (hg + 1))
                if u == 0:
                    pe.wait_ge(floor_ready, 2 * p + 2)
                for blk in range(BLKS):
                    if u > 0:
                        pe.wait_ge(prod_done, BLKS * UNITS * p + BLKS * (u - 1) + blk + 1)
                    elif q is not None:
                        pe.wait_ge(*((t_ready, 4 * FT * q + 1), (acc_ready, 4 * FT * q + 1))[blk])
                    t0 = b * S + blk * P
                    pe.matmul(pq[:, 2 * blk], xT[:, KT + hg, t0:t0 + P],
                              q_diag[:, hg % 2, :, t0:t0 + P], start=True, stop=True).then_inc(qk_done, 1)

            def state_sums(p, q, u):
                hg, b = u // 2, u % 2
                pe.wait_ge(vw_ready, UNITS * p + u + 1)
                if u > 0:
                    pe.wait_ge(later_ready, UNITS * p + u)
                elif q is not None:
                    pe.wait_ge(t_ready, 4 * FT * q + 2)
                pe.matmul(pq[:, 1, 0:HG * (DH + 1)], ctx_sb[:, 2 * b, hg * P:(hg + 1) * P],
                          vw[:, u % 2].rearrange("q h d -> q (h d)"), start=True, stop=True
                          ).then_inc(st_done, 1)

            def values(p, q, u):
                hg, b = u // 2, u % 2
                if u == 0 and q is not None:
                    pe.wait_ge(acc_ready, 4 * FT * q + 2)
                if u == 0:
                    pe.wait_ge(v_ready, TT * p + TT)
                if u > 0:
                    pe.wait_ge(o_read, UNITS * p + u)
                elif not (isinstance(p, int) and p == 0):
                    pe.wait_ge(o_read, UNITS * p)
                for s in range(2):
                    pe.wait_ge(prod_done, BLKS * UNITS * p + BLKS * u + 1 + s)
                    for h in range(HG):
                        pe.matmul(po[:, (s * HG + h) * (DH + 1):(s * HG + h + 1) * (DH + 1)],
                                  dmat[:, u % 2, s, h], v_sb[:, 2 * b + s, hg * HG + h],
                                  start=True, stop=True)
                pe.wait_ge(state_ready, UNITS * p + u + 1)
                pe.matmul(pq[:, 1, HG * (DH + 1):2 * HG * (DH + 1)], xT[:, hg, b * S + P:(b + 1) * S],
                          state[:, u % 2].rearrange("q h d -> q (h d)"), start=True, stop=True
                          ).then_inc(pv_done, 1)

            def turn_y(p):
                pe.wait_ge(yn_ready, p + 1)
                if isinstance(p, int) and p == 0:
                    pe.wait_ge(xT_read, 2 * KT * 2)
                else:
                    pe.wait_ge(prod_done, BLKS * UNITS * (p + 1))
                    pe.wait_ge(o_read, UNITS * (p + 1))
                    pe.wait_ge(acc_ready, 4 * FT * p)
                for n in range(KT):
                    if n >= 2:
                        pe.wait_ge(yh_ready, KT * p + n - 1)
                        pe.wait_ge(yl_ready, KT * p + n - 1)
                    for tt in range(TT):
                        last = pe.transpose(bank_y(p, n)[:, tt * P:(tt + 1) * P],
                                            yn[:, tt, n * P:(n + 1) * P], ident[:])
                    last.then_inc(yT_done, 1)

            def ffn_up(q, h):
                if h == 0:
                    pe.wait_ge(yh_ready, KT * q + KT)
                    pe.wait_ge(yl_ready, KT * q + KT)
                prev = h - 1 if h and spare(q, h - 1) == spare(q, h) else h - 2
                if spare(q, h) and h == 0:
                    pe.wait_ge(xT_read, 2 * KT * (q + 2))
                    pe.wait_ge(floor_ready, 2 * (q + 2))
                    pe.wait_ge(o_read, UNITS * (q + 1))
                elif spare(q, h) and (prev < 0 or not spare(q, prev)):
                    pairs = PAIRS if isinstance(q, int) and q == PAIRS - 1 else q + 2
                    pe.wait_ge(prod_done, BLKS * UNITS * pairs)
                    pe.wait_ge(later_ready, UNITS * pairs)
                    pe.wait_ge(o_read, UNITS * pairs)
                for g in range(KT):
                    if spare(q, h) and (prev < 0 or not spare(q, prev)):
                        pass
                    elif prev < 0 or spare(q, prev) != spare(q, h):
                        pe.wait_ge(o_ready, TT * q + g + 1)
                    elif g < 2:
                        pe.wait_ge(t_ready, 4 * FT * q + 2 * prev + 1 + g)
                    else:
                        pe.wait_ge(acc_ready, 4 * FT * q + 2 * prev - 1 + g)
                    for part in range(2):
                        last = pe.matmul(bank(q, h, g), gu_val[:, h // 2 + h % 2 * FT, g], yT[:, part, g],
                                         start=(part == 0), stop=(part == 1))
                    last.then_inc(pu_done, 1)

            def down(q, tt, js):
                if tt == 0 and js[0] == 0:
                    pe.wait_ge(t_ready, 4 * FT * (q + 1) - 2)
                if tt == 2 and js[0] == 0:
                    pe.wait_ge(acc_ready, 4 * FT * (q + 1) - 2)
                for j in js:
                    if tt == 0:
                        pe.wait_ge(h_ready, FT * q + j + 1)
                    last = pe.matmul(pf[:, tt], hT[:, j, tt * P:(tt + 1) * P], w_down[:, j],
                                     start=(j == 0), stop=(j == FT - 1))
                if js[-1] == FT - 1:
                    last.then_inc(dn_done, 1)

            def prepare(j):
                if j == 0:
                    pe.wait_ge(const_ready, 6)
                    pe.wait_ge(s_const, 16 * 7)
                    pe.transpose(pf[:, 0].bitcast(F16)[:, 0:KT * GU], sc_raw[:], ident16[0:KT * GU, 0:KT * GU])
                    pe.transpose(pf[:, 1].bitcast(F16)[:, 0:FT * KT], dsc_raw[:],
                                 ident16[0:FT * KT, 0:FT * KT]).then_inc(sc_done, 1)
                for n in GU_PREP.get(j, ()):
                    if n == 0:
                        pe.wait_ge(sc_ready, 3)
                    pe.wait_ge(fp4_ready, 1 if 2 * n + 1 < FT else 2)
                    if n >= 4:
                        pe.wait_ge(gut_read, n - 3)
                    for o in range(2):
                        for g in range(KT):
                            k = (o * KT + g) * P
                            last = pe.transpose(
                                pf[:, n % 4].bitcast(F16)[:, k:k + P],
                                gu_fp4[:, 2 * n + o, g * P:(g + 1) * P],
                                ident16[:])
                    last.then_inc(gut_done, 1)
                for n in DN_PREP.get(j, ()):
                    if n == 0:
                        pe.wait_ge(dn32_ready, 4 * KT)
                        pe.wait_ge(gut_read, FT)
                    if n >= 4:
                        pe.wait_ge(dnt_read, n - 3)
                    for o in range(KT):
                        last = pe.transpose(
                            pf[:, n % 4, o * P:(o + 1) * P],
                            dn_f32[:, o, n * P:(n + 1) * P],
                            ident[:])
                    last.then_inc(dnt_done, 1)

            def iteration(p, q, n):
                for h in range(GU):
                    if q is not None:
                        ffn_up(q, h)
                    elif h % 2 == 0 and h > 0:
                        prepare(h // 2)
                    if p is not None:
                        if q is None and h in VALUES and VALUES[h] + 1 < UNITS:
                            scores(p, q, VALUES[h] + 1)
                        if h in VALUES:
                            values(p, q, VALUES[h])
                            if q is None and VALUES[h] + 1 < UNITS:
                                state_sums(p, q, VALUES[h] + 1)
                        if h in SCORES and (q is not None or SCORES[h] == 0):
                            scores(p, q, SCORES[h])
                            state_sums(p, q, SCORES[h])
                if q is not None:
                    down(q, 0, range(FT))
                    down(q, 1, range(FT))
                    down(q, 2, range(BEFORE_TURNS))
                if n is not None:
                    turn_x(n, 0)
                if p is not None and q is not None:
                    turn_y(p)
                if n is not None:
                    turn_x(n, 1)
                    gate_sums(n)
                if q is not None:
                    down(q, 2, range(BEFORE_TURNS, FT))
                    down(q, 3, range(BEFORE_BACK))
                if q is None:
                    turn_y(p)
                if n is not None:
                    turn_back(n)
                if q is not None:
                    down(q, 3, range(BEFORE_BACK, FT))

            pe.wait_ge(const_ready, 6)
            turn_x(0, 0)
            turn_x(0, 1)
            gate_sums(0)
            prepare(0)
            turn_back(0)
            iteration(0, None, 1)
            pe.wait_ge(dnt_read, FT)
            with pe.Fori(1, PAIRS - 1) as p:
                iteration(p, p - 1, p + 1)
            iteration(PAIRS - 1, PAIRS - 2, None)
            iteration(None, PAIRS - 1, None)

        @block.vector
        def _(dve):
            g1, g2, po_steps = Chain(dve, dve_g1), Chain(dve, dve_g2), Chain(dve, dve_p)

            def stats(chain, src, k, tt):
                chain.link(dve.bn_stats(bst[:, k, tt], src))
                take_wait(dve)
                chain.inc(dve.bn_aggr(mv[:, k, tt], bst[:, k, tt]))

            def norm1_sums(p, tiles=range(TT)):
                if tiles[0] == 0:
                    g1.start(p)
                    dve.wait_ge(s_xg, 16 * p + 16)
                for tt in tiles:
                    stats(g1, xg[:, tt], 0, tt)
                if tiles[-1] < TT - 1:
                    return
                g1.wait()
                dve.tensor_scalar(vv[:, 0], mv[:, 0, :, 1], EPS_LN, None, ALU.add).then_inc(var1_ready, 1)

            def norm1(p):
                dve.wait_ge(rstd1_ready, p + 1)
                for tt in range(TT):
                    last = dve.tensor_scalar(xg[:, tt], xg[:, tt], mv[:, 0, tt, 0:1], rs[:, 0, tt:tt + 1],
                                             ALU.subtract, ALU.mult)
                last.then_inc(xn_ready, 1)

            def v_means(p):
                dve.wait_ge(s_ctx, 16 * p + 16)
                g1.link(dve.tensor_reduce(vmean[:, 0], ctx_sb[:].rearrange("q t (h d) -> q (t h) d", d=DH),
                                       AX.X, ALU.add))
                dve.tensor_scalar(vmean[:, 1], vmean[:, 0], -1.0 / DH, None, ALU.mult).then_inc(vmean_ready, 1)

            def spread_q(p, hg):
                dve.wait_ge(xT_read, 2 * KT * p + KT + hg + 1)
                if isinstance(p, int) and p == 0 and hg == 0:
                    dve.wait_ge(const_ready, 10)
                if hg >= 2:
                    dve.wait_ge(qk_done, BLKS * (UNITS * p + 2 * (hg - 1)))
                for h in range(HG):
                    r = slice(h * DH, (h + 1) * DH)
                    dve.tensor_copy(q_diag[r, hg % 2, h], xT[r, hg]).then_inc(qdiag_ready, 1)

            def gate_rows(p):
                g2.start(p)
                dve.wait_ge(g_done, p + 1)
                if isinstance(p, int) and p == 0:
                    dve.wait_ge(s_const, 16 * 7)
                f = slice(DH, DH + NH)
                g2.link(dve.tensor_scalar(gates[:, 1], pm[f, :], bias_col[f], None, ALU.add))
                dve.scalar_tensor_tensor(lf[:, 0], gates[:, 1], -1.0, gates[:, 1], ALU.mult, ALU.max
                                         ).then_inc(absf_ready, 1)
                g2.link(dve.tensor_scalar(gates[:, 0], pm[0:NH, :], bias_col[0:NH], None, ALU.add))

            def scans(p):
                dve.wait_ge(softp_ready, p + 1)
                g2.link(dve.scalar_tensor_tensor(lf[:, 3], gates[:, 1], 0.0, lf[:, 2], ALU.min, ALU.subtract))
                batches = slice(0, S), slice(S, 2 * S)
                for b in batches:
                    g2.inc(dve.tensor_tensor_scan(lf[:, 1, b], lf[:, 3, b], lf[:, 3, b], 0.0, ALU.add, ALU.min))
                g2.wait()
                ins = dve.tensor_tensor(am[:, 0], gates[:, 0], lf[:, 1], ALU.subtract)
                ins.then_inc(am_ready, 1)
                dve.wait_ge(am_ready, 2 * p + 1)
                for b in batches:
                    g2.inc(dve.tensor_tensor_scan(lf[:, 2, b], am[:, 0, b], am[:, 0, b], -3.0e38,
                                                  ALU.max, ALU.max))
                g2.wait()
                if not (isinstance(p, int) and p == 0):
                    dve.wait_ge(s_nm, 16 * p)
                dve.tensor_scalar(nm[:], lf[:, 2], -1.0, None, ALU.mult).then_inc(nm_ready, 1)
                dve.wait_ge(nm_ready, p + 1)
                for b in range(2):
                    c = slice(b * S + P, (b + 1) * S)
                    g2.inc(dve.tensor_scalar(lf[:, 0, c], nm[:, c], nm[:, b * S + P - 1:b * S + P], None,
                                             ALU.subtract))
                g2.wait()
                dve.scalar_tensor_tensor(am[:, 1], lf[:, 2], -1.0, lf[:, 1], ALU.mult, ALU.subtract
                                         ).then_inc(am_ready, 1)

            def read_a(p):
                dve.wait_ge(back_done, p + 1)
                dve.tensor_copy(aT[:].rearrange("q c n -> q (c n)"), pm[:, 0:4 * NH]).then_inc(aT_ready, 1)

            def products(p, u, blks):
                for blk in blks:
                    if blk == 0:
                        dve.wait_ge(mask_done, 2 * UNITS * p + 2 * u + 2)
                        dve.wait_ge(vw_ready, UNITS * p + u + 1)
                    dve.wait_ge(qk_done, BLKS * UNITS * p + BLKS * u + blk + 1)
                    d = dmat[:, u % 2, blk].rearrange("q h s -> q (h s)")
                    dve.scalar_tensor_tensor(d, pq[:, 2 * blk], float(DH) ** -0.5, d, ALU.mult, ALU.mult
                                             ).then_inc(prod_done, 1)

            def keep_state(p, u):
                dve.wait_ge(st_done, UNITS * p + u + 1)
                dve.tensor_tensor(state[:, u % 2], pq[:, 1, 0:HG * (DH + 1)].rearrange(
                    "q (h d) -> q h d", h=HG), own_rows[:], ALU.mult).then_inc(state_ready, 1)

            def later_part(p, u):
                hg, b = u // 2, u % 2
                dve.wait_ge(pv_done, UNITS * p + u + 1)
                if u == 0:
                    dve.wait_ge(floor_ready, 2 * p + 2)
                dve.tensor_tensor(later[:, u % 2], pq[:, 1, HG * (DH + 1):2 * HG * (DH + 1)].rearrange(
                                      "q (h d) -> q h d", h=HG),
                                  decay[:, b, hg * HG:(hg + 1) * HG].unsqueeze(2).to_broadcast(
                                      [P, HG, DH + 1]), ALU.mult).then_inc(later_ready, 1)

            def add_later(p, u):
                hg, b = u // 2, u % 2
                dve.wait_ge(o_read, UNITS * p + u + 1)
                dve.wait_ge(later_ready, UNITS * p + u + 1)
                o = tok[:, 2 * b + 1, hg * HG:(hg + 1) * HG, :]
                dve.tensor_tensor(o, o, later[:, u % 2], ALU.add).then_inc(o_whole, 1)

            def post(p):
                link = po_steps.link
                po_steps.start(p)
                sums = tok[:].rearrange("q t h d -> q (t h) d")
                dve.wait_ge(o_whole, UNITS * p + UNITS)
                link(dve.scalar_tensor_tensor(hn[:, 0], sums[:, :, DH], -1.0, sums[:, :, DH],
                                              ALU.mult, ALU.max))
                link(dve.tensor_tensor(hn[:, 1], hn[:, 0], floor[:].rearrange("q b c h -> q (b c h)"),
                                       ALU.max))
                link(dve.tensor_scalar(hn[:, 1], hn[:, 1], EPS, None, ALU.add))
                link(dve.tensor_tensor(hn[:, 2], hn[:, 1], hn[:, 1], ALU.mult))
                dve.wait_ge(osq_ready, 2 * p + 2)
                link(dve.tensor_reduce(hn[:, 0], osq, AX.X, ALU.add))
                link(dve.tensor_scalar(hn[:, 1], hn[:, 0], 1.0 / DH, None, ALU.mult))
                dve.scalar_tensor_tensor(hn[:, 3], hn[:, 2], EPS, hn[:, 1], ALU.mult, ALU.add
                                         ).then_inc(hvar_ready, 1)
                dve.wait_ge(hvar_ready, p + 1)
                link(dve.tensor_scalar(hn[:, 3], hn[:, 3], VAR_MAX, None, ALU.min))
                link(dve.tensor_scalar(hn[:, 0].bitcast(I32), hn[:, 3].bitcast(I32), 1, None,
                                       ALU.logical_shift_right))
                link(dve.tensor_scalar(hr[:].bitcast(I32), hn[:, 0].bitcast(I32), -1.0, RSQRT_START,
                                       ALU.mult, ALU.add))
                for _ in range(3):
                    link(dve.tensor_tensor(hn[:, 0], hr[:], hr[:], ALU.mult))
                    link(dve.scalar_tensor_tensor(hn[:, 1], hn[:, 0], -0.5, hn[:, 3], ALU.mult, ALU.mult))
                    link(dve.scalar_tensor_tensor(hr[:], hn[:, 1], 1.5, hr[:], ALU.add, ALU.mult))
                for tt in range(TT):
                    dve.wait_ge(ols_ready, TT * p + tt + 1)
                    o = tok[:, tt, :, 0:DH]
                    r = hr[:, tt * NH:(tt + 1) * NH].unsqueeze(2).to_broadcast([P, NH, DH])
                    dve.tensor_tensor(o, o, r, ALU.mult).then_inc(oscaled, 1)

            def norm2_sums(p):
                for tt in range(TT):
                    dve.wait_ge(x1_ready, TT * p + tt + 1)
                    stats(po_steps, x_sb[:, tt], 1, tt)
                po_steps.wait()
                dve.tensor_scalar(vv[:, 1], mv[:, 1, :, 1], EPS_LN, None, ALU.add).then_inc(var2_ready, 1)

            def norm2(p):
                dve.wait_ge(rstd2_ready, p + 1)
                po_steps.link(dve.tensor_scalar(rk[:], rs[:, 1], PX, None, ALU.mult))
                for tt in range(TT):
                    last = dve.tensor_scalar(yn[:, tt].rearrange("q (w i h) -> q w h i", i=4, h=2),
                                             x_sb[:, tt].rearrange("q (w h i) -> q w h i", i=4, h=2),
                                             mv[:, 1, tt, 0:1], rk[:, tt:tt + 1], ALU.subtract, ALU.mult)
                last.then_inc(yn_ready, 1)

            def low_yT(p):
                for n in range(KT):
                    dve.wait_ge(yh_ready, KT * p + n + 1)
                    dve.tensor_tensor(yT[:, 1, n], bank_y(p, n), yT[:, 0, n], ALU.subtract
                                      ).then_inc(yl_ready, 1)

            def ffn_up(q, h, p, u):
                j, w = h // 2, h % 2
                o = j + w * FT
                if u is not None:
                    products(p, u, (0,))
                acc = ffn[:, 4 + 2 * w + j % 2]
                if w == 1 and j >= 2:
                    dve.wait_ge(h_ready, FT * q + j - 1)
                dve.wait_ge(tsum_ready, 2 * FT * q + h + 1)
                dve.wait_ge(pu_done, 8 * FT * q + 4 * h + 3)
                dve.scalar_tensor_tensor(acc, bank(q, h, 2), gu_scale[:, 2 * GU + o:2 * GU + o + 1],
                                         ffn[:, 2 * w], ALU.mult, ALU.add).then_inc(acc_ready, 1)
                dve.wait_ge(pu_done, 8 * FT * q + 4 * h + 4)
                dve.wait_ge(acc_ready, 4 * FT * q + 2 * h + 1)
                dve.scalar_tensor_tensor(acc, bank(q, h, 3), gu_scale[:, 3 * GU + o:3 * GU + o + 1],
                                         acc, ALU.mult, ALU.add).then_inc(acc_ready, 1)
                if u is not None:
                    products(p, u, (1,))
                    keep_state(p, u)

            def gate(q, j):
                dve.wait_ge(th_ready, FT * q + j + 1)
                dve.scalar_tensor_tensor(th[:, j % 2], th[:, j % 2], 1.0, ffn[:, 4 + j % 2],
                                         ALU.add, ALU.mult).then_inc(gg_ready, 1)

            def down(q, part):
                tiles = PARTS[part]
                c = slice(tiles[0], tiles[-1] + 1)
                dve.wait_ge(ss_ready, TT * q + tiles[-1] + 1)
                dve.tensor_scalar(ms[:, c], ssq[:, c], 1.0 / E, EPS, ALU.mult, ALU.add).then_inc(ms_ready, 1)
                dve.wait_ge(yr_ready, 3 * q + part + 1)
                dve.wait_ge(s_res, 16 * q + 16)
                for tt in tiles:
                    dve.scalar_tensor_tensor(x_res[:, tt], pf[:, tt], yr[:, tt:tt + 1], x_res[:, tt],
                                             ALU.mult, ALU.add).then_inc(o_ready, 1)

            own = [0]

            def step(ins):
                ins.then_inc(dve_w, 1)
                own[0] += 1
                dve.wait_ge(dve_w, own[0])

            def decode(words, dst, a, bb, i):
                step(dve.tensor_scalar(a, words, 12 - 4 * i, SIGN_MASK, ALU.logical_shift_left,
                                       ALU.bitwise_and))
                if i < 3:
                    step(dve.tensor_scalar(bb, words, 9 - 4 * i, MAGN_MASK, ALU.logical_shift_left,
                                           ALU.bitwise_and))
                else:
                    step(dve.tensor_scalar(bb, words, 3, MAGN_MASK, ALU.logical_shift_right,
                                           ALU.bitwise_and))
                step(dve.tensor_tensor(dst(i), a, bb, ALU.bitwise_or))
                if i == 3:
                    dve.sem_inc(fp4_ready, 1)

            def gate_weights():
                dve.wait_ge(s_const, 16 * 7)
                dve.wait_ge(const_ready, 10)
                dve.tensor_tensor(w_gate[:, KT:2 * KT], w_gate[:, KT:2 * KT], w_gate[:, 2 * KT:3 * KT],
                                  ALU.add).then_inc(wg_ready, 1)

            def prepare_up(j):
                dve.wait_ge(s_words, 32)
                o = slice(j * FT, (j + 1) * FT)
                a, bb = (bits[:, k * FT * NW:(k + 1) * FT * NW].rearrange("q (o w) -> q o w", o=FT)
                         for k in range(2))
                for i in range(4):
                    decode(gu_words[:, o], lambda i: gu_bits[:, o, :, i], a, bb, i)

            def prepare_down(j):
                if j < 4:
                    dve.wait_ge(xT_done, 2 * KT)
                    a, bb = (bits[:, k * KT * DW:(k + 1) * KT * DW].rearrange("q (o w) -> q o w", o=KT)
                             for k in range(2))
                    decode(dn_words, lambda i: dn_bits[:, :, :, i], a, bb, j)
                    return
                if j == 4:
                    dve.wait_ge(gut_done, FT)
                    dve.wait_ge(sc_ready, 3)
                o = j - 4
                for i in range(4):
                    s = dn_scale[:].rearrange("q (g o) -> q g o", o=KT)[:, :, o]
                    dve.tensor_tensor(
                        dn_f32[:, o].rearrange("q (g w h i) -> q i g w h", g=FT, h=2, i=4)[:, i],
                        dn_fp4[:, o, i], s.unsqueeze(2).unsqueeze(3).to_broadcast([P, FT, 16, 2]),
                        ALU.mult).then_inc(dn32_ready, 1)

            def iteration(p, q, n):
                for h in range(GU):
                    u = SCORES.get(h) if p is not None else None
                    if u is not None and q is None:
                        products(p, u, range(BLKS))
                        keep_state(p, u)
                    if q is not None:
                        if h % 2 == 0 and h > 0:
                            gate(q, h // 2 - 1)
                        ffn_up(q, h, p, u)
                    elif DN_WORDS_AT <= h < DN_WORDS_AT + 8:
                        prepare_down(h - DN_WORDS_AT)
                    if p is not None and h in VALUES:
                        later_part(p, VALUES[h])
                    if p is not None and h in ADD:
                        add_later(p, ADD[h])
                    if p is not None and h in SPREAD:
                        spread_q(p, SPREAD[h])
                    if q is None and 11 <= h < 11 + TT:
                        norm1_sums(n, (h - 11,))
                    if q is None and h == 11 + TT:
                        norm1(n)
                if q is None:
                    post(p)
                    v_means(n)
                    norm2_sums(p)
                    gate_rows(n)
                    norm2(p)
                    scans(n)
                    low_yT(p)
                    read_a(n)
                    spread_q(n, 0)
                    spread_q(n, 1)
                    return
                if q is not None:
                    gate(q, FT - 1)
                if p is not None:
                    post(p)
                if n is not None:
                    norm1_sums(n)
                if p is not None:
                    norm2_sums(p)
                if n is not None:
                    norm1(n)
                if p is not None:
                    norm2(p)
                    low_yT(p)
                if q is not None:
                    down(q, 0)
                if n is not None:
                    v_means(n)
                    spread_q(n, 0)
                    spread_q(n, 1)
                    gate_rows(n)
                    scans(n)
                if q is not None:
                    down(q, 1)
                if n is not None:
                    read_a(n)
                if q is not None:
                    down(q, 2)

            norm1_sums(0)
            norm1(0)
            v_means(0)
            gate_weights()
            prepare_up(0)
            gate_rows(0)
            spread_q(0, 0)
            scans(0)
            spread_q(0, 1)
            read_a(0)
            prepare_up(1)
            iteration(0, None, 1)
            dve.sem_inc(o_ready, TT)
            with dve.Fori(1, PAIRS - 1) as p:
                iteration(p, p - 1, p + 1)
            iteration(PAIRS - 1, PAIRS - 2, None)
            iteration(None, PAIRS - 1, None)


_INS = ["x", "ctx_2048", "L0_xattn_Wi", "L0_xattn_bi", "L0_xattn_Wf", "L0_xattn_bf", "L0_xattn_ln_scale",
        "L0_ffn_gate_up_packed", "L0_ffn_gate_up_scales", "L0_ffn_down_packed", "L0_ffn_down_scales"]


def kernel(**inputs):
    import numpy as _np
    import concourse.bacc as _bacc
    from concourse import mybir as _mybir
    from concourse.bass_utils import run_bass_kernel_spmd as _run

    nc = _bacc.Bacc("TRN2", target_bir_lowering=False, num_devices=1)
    arrays, args = {}, []
    for name in _INS:
        a = _np.ascontiguousarray(inputs[name])
        arrays[f"in_{name}"] = a
        args.append(nc.dram_tensor(f"in_{name}", a.shape, _mybir.dt.from_np(a.dtype), kind="ExternalInput").ap())
    args.append(nc.dram_tensor("out_0", (B, S, E), F32, kind="ExternalOutput").ap())
    xattn_ffn(nc, *args)
    r = _run(nc, [arrays], core_ids=[0])
    return r.results[0]["out_0"]
```
